# Optimizing a Trainium2 kernel written in Bass

```python
import numpy as np
import jax
import jax.numpy as jnp

def _softmax(x, axis=-1):
    return jax.nn.softmax(x, axis=axis)

def _gelu(x):
    return jax.nn.gelu(x, approximate=True)

def _silu(x):
    return jax.nn.silu(x)

def _sigmoid(x):
    return jax.nn.sigmoid(x)

def _layernorm(x, axis=-1, eps=1e-05):
    m = jnp.mean(x, axis=axis, keepdims=True)
    v = jnp.var(x, axis=axis, keepdims=True)
    return (x - m) / jnp.sqrt(v + eps)

def _scatter_add(tgt, idx, src, axis=0):
    return tgt.at[idx].add(src)

def _segment_sum(src, seg, n):
    return jax.ops.segment_sum(src, seg, n)
kernel_name = 'mk_seq_preln_d1_jaxref_r4_84cfb2'

def setup_inputs(seed: int=0):
    np.random.seed(seed)
    _w = jnp.asarray

    def _L0_attn_setup():
        import jax, jax.numpy as jnp
        import numpy as np
        DIM = 256
        HEADS = 16
        HEAD_DIM = DIM // HEADS
        RADIUS = 7
        WIN = 2 * RADIUS + 1
        HIDDEN = 4 * DIM
        B, L = (2, 512)
        EPS = 1e-05

        def _layernorm(x, g, b):
            mu = jnp.mean(x, axis=-1, keepdims=True)
            var = jnp.mean(jnp.square(x - mu), axis=-1, keepdims=True)
            return (x - mu) * jax.lax.rsqrt(var + EPS) * g + b

        def _neighborhood_attn(xn, qkv_w, qkv_b, proj_w, proj_b):
            Bz, Lz, _ = xn.shape
            qkv = xn @ qkv_w + qkv_b
            qkv = qkv.reshape(Bz, Lz, 3, HEADS, HEAD_DIM)
            q = qkv[:, :, 0].transpose(0, 2, 1, 3).reshape(Bz * HEADS, Lz, HEAD_DIM)
            k = qkv[:, :, 1].transpose(0, 2, 1, 3).reshape(Bz * HEADS, Lz, HEAD_DIM)
            v = qkv[:, :, 2].transpose(0, 2, 1, 3).reshape(Bz * HEADS, Lz, HEAD_DIM)
            k_pad = jnp.pad(k, ((0, 0), (RADIUS, RADIUS), (0, 0)))
            v_pad = jnp.pad(v, ((0, 0), (RADIUS, RADIUS), (0, 0)))
            idx = jnp.arange(Lz)[:, None] + jnp.arange(WIN)[None, :]
            kw = k_pad[:, idx]
            vw = v_pad[:, idx]
            scale = np.sqrt(HEAD_DIM).astype(np.float32)
            scores = jnp.einsum('bld,blwd->blw', q, kw) / scale
            attn = jax.nn.softmax(scores, axis=-1)
            out = jnp.einsum('blw,blwd->bld', attn, vw)
            out = out.reshape(Bz, HEADS, Lz, HEAD_DIM).transpose(0, 2, 1, 3).reshape(Bz, Lz, DIM)
            return out @ proj_w + proj_b
        key = jax.random.key(seed)
        ks = jax.random.split(key, 12)
        s = lambda fan_in: 1.0 / np.sqrt(fan_in)
        return {'x': jax.random.normal(ks[0], (B, L, DIM), dtype=jnp.float32), 'qkv_w': jax.random.uniform(ks[1], (DIM, 3 * DIM), jnp.float32, -s(DIM), s(DIM)), 'qkv_b': jax.random.uniform(ks[2], (3 * DIM,), jnp.float32, -s(DIM), s(DIM)), 'proj_w': jax.random.uniform(ks[3], (DIM, DIM), jnp.float32, -s(DIM), s(DIM)), 'proj_b': jax.random.uniform(ks[4], (DIM,), jnp.float32, -s(DIM), s(DIM)), 'norm1_g': jnp.ones((DIM,), jnp.float32), 'norm1_b': jnp.zeros((DIM,), jnp.float32), 'norm2_g': jnp.ones((DIM,), jnp.float32), 'norm2_b': jnp.zeros((DIM,), jnp.float32), 'fc1_w': jax.random.uniform(ks[5], (DIM, HIDDEN), jnp.float32, -s(DIM), s(DIM)), 'fc1_b': jax.random.uniform(ks[6], (HIDDEN,), jnp.float32, -s(DIM), s(DIM)), 'fc2_w': jax.random.uniform(ks[7], (HIDDEN, DIM), jnp.float32, -s(HIDDEN), s(HIDDEN)), 'fc2_b': jax.random.uniform(ks[8], (DIM,), jnp.float32, -s(HIDDEN), s(HIDDEN))}
    _L0_attn_in = _L0_attn_setup()

    def _L0_ffn_setup():
        import jax, jax.numpy as jnp
        import numpy as np
        from jax import lax
        B, N, D, H, E, K = (16, 256, 256, 1024, 8, 2)
        key = jax.random.key(seed)
        ks = jax.random.split(key, 12)
        s = 0.02
        return {'x': jax.random.normal(ks[0], (B, N, D), jnp.float32), 'alpha': jnp.asarray(0.9, jnp.float32), 'w_gate': jax.random.normal(ks[1], (D, E), jnp.float32) * s, 'b_gate': jnp.zeros((E,), jnp.float32), 'W1m': jax.random.normal(ks[2], (D, H), jnp.float32) * s, 'b1m': jnp.zeros((H,), jnp.float32), 'W2m': jax.random.normal(ks[3], (H, D), jnp.float32) * s, 'b2m': jnp.zeros((D,), jnp.float32), 'W1e': jax.random.normal(ks[4], (E, D, H), jnp.float32) * s, 'b1e': jnp.zeros((E, H), jnp.float32), 'W2e': jax.random.normal(ks[5], (E, H, D), jnp.float32) * s, 'b2e': jnp.zeros((E, D), jnp.float32)}
    _L0_ffn_in = _L0_ffn_setup()
    _d = {'L0_attn_x': _L0_attn_in['x'], 'L0_attn_qkv_w': _L0_attn_in['qkv_w'], 'L0_attn_qkv_b': _L0_attn_in['qkv_b'], 'L0_attn_proj_w': _L0_attn_in['proj_w'], 'L0_attn_proj_b': _L0_attn_in['proj_b'], 'L0_attn_norm1_g': _L0_attn_in['norm1_g'], 'L0_attn_norm1_b': _L0_attn_in['norm1_b'], 'L0_attn_norm2_g': _L0_attn_in['norm2_g'], 'L0_attn_norm2_b': _L0_attn_in['norm2_b'], 'L0_attn_fc1_w': _L0_attn_in['fc1_w'], 'L0_attn_fc1_b': _L0_attn_in['fc1_b'], 'L0_attn_fc2_w': _L0_attn_in['fc2_w'], 'L0_attn_fc2_b': _L0_attn_in['fc2_b'], 'L0_ffn_alpha': _L0_ffn_in['alpha'], 'L0_ffn_w_gate': _L0_ffn_in['w_gate'], 'L0_ffn_b_gate': _L0_ffn_in['b_gate'], 'L0_ffn_W1m': _L0_ffn_in['W1m'], 'L0_ffn_b1m': _L0_ffn_in['b1m'], 'L0_ffn_W2m': _L0_ffn_in['W2m'], 'L0_ffn_b2m': _L0_ffn_in['b2m'], 'L0_ffn_W1e': _L0_ffn_in['W1e'], 'L0_ffn_b1e': _L0_ffn_in['b1e'], 'L0_ffn_W2e': _L0_ffn_in['W2e'], 'L0_ffn_b2e': _L0_ffn_in['b2e']}
    _x0 = _d['L0_attn_x']
    _d['L0_attn_x'] = jax.random.normal(jax.random.fold_in(jax.random.key(seed), 1), (16, 512, 256), dtype=_x0.dtype)
    del _x0
    return _d

def reference(L0_attn_x, L0_attn_qkv_w, L0_attn_qkv_b, L0_attn_proj_w, L0_attn_proj_b, L0_attn_norm1_g, L0_attn_norm1_b, L0_attn_norm2_g, L0_attn_norm2_b, L0_attn_fc1_w, L0_attn_fc1_b, L0_attn_fc2_w, L0_attn_fc2_b, L0_ffn_alpha, L0_ffn_w_gate, L0_ffn_b_gate, L0_ffn_W1m, L0_ffn_b1m, L0_ffn_W2m, L0_ffn_b2m, L0_ffn_W1e, L0_ffn_b1e, L0_ffn_W2e, L0_ffn_b2e):

    def _L0_attn_ref(x, qkv_w, qkv_b, proj_w, proj_b, norm1_g, norm1_b, norm2_g, norm2_b, fc1_w, fc1_b, fc2_w, fc2_b):
        import jax, jax.numpy as jnp
        import numpy as np
        DIM = 256
        HEADS = 16
        HEAD_DIM = DIM // HEADS
        RADIUS = 7
        WIN = 2 * RADIUS + 1
        HIDDEN = 4 * DIM
        B, L = (2, 512)
        EPS = 1e-05

        def _layernorm(x, g, b):
            mu = jnp.mean(x, axis=-1, keepdims=True)
            var = jnp.mean(jnp.square(x - mu), axis=-1, keepdims=True)
            return (x - mu) * jax.lax.rsqrt(var + EPS) * g + b

        def _neighborhood_attn(xn, qkv_w, qkv_b, proj_w, proj_b):
            Bz, Lz, _ = xn.shape
            qkv = xn @ qkv_w + qkv_b
            qkv = qkv.reshape(Bz, Lz, 3, HEADS, HEAD_DIM)
            q = qkv[:, :, 0].transpose(0, 2, 1, 3).reshape(Bz * HEADS, Lz, HEAD_DIM)
            k = qkv[:, :, 1].transpose(0, 2, 1, 3).reshape(Bz * HEADS, Lz, HEAD_DIM)
            v = qkv[:, :, 2].transpose(0, 2, 1, 3).reshape(Bz * HEADS, Lz, HEAD_DIM)
            k_pad = jnp.pad(k, ((0, 0), (RADIUS, RADIUS), (0, 0)))
            v_pad = jnp.pad(v, ((0, 0), (RADIUS, RADIUS), (0, 0)))
            idx = jnp.arange(Lz)[:, None] + jnp.arange(WIN)[None, :]
            kw = k_pad[:, idx]
            vw = v_pad[:, idx]
            scale = np.sqrt(HEAD_DIM).astype(np.float32)
            scores = jnp.einsum('bld,blwd->blw', q, kw) / scale
            attn = jax.nn.softmax(scores, axis=-1)
            out = jnp.einsum('blw,blwd->bld', attn, vw)
            out = out.reshape(Bz, HEADS, Lz, HEAD_DIM).transpose(0, 2, 1, 3).reshape(Bz, Lz, DIM)
            return out @ proj_w + proj_b
        shortcut = x
        h = _layernorm(x, norm1_g, norm1_b)
        h = _neighborhood_attn(h, qkv_w, qkv_b, proj_w, proj_b)
        x = shortcut + h
        m = _layernorm(x, norm2_g, norm2_b)
        m = jax.nn.gelu(m @ fc1_w + fc1_b, approximate=False) @ fc2_w + fc2_b
        return x + m

    def _L0_ffn_ref(x, alpha, w_gate, b_gate, W1m, b1m, W2m, b2m, W1e, b1e, W2e, b2e):
        import jax, jax.numpy as jnp
        import numpy as np
        from jax import lax
        B, N, D, H, E, K = (16, 256, 256, 1024, 8, 2)
        main = jax.nn.gelu(x @ W1m + b1m) @ W2m + b2m
        logits = jnp.mean(x, axis=1) @ w_gate + b_gate
        probs = jax.nn.softmax(logits, axis=-1)
        top_vals, top_idx = lax.top_k(probs, K)
        gate_w = top_vals / jnp.sum(top_vals, axis=-1, keepdims=True)
        W1g = W1e[top_idx]
        b1g = b1e[top_idx]
        W2g = W2e[top_idx]
        b2g = b2e[top_idx]
        h = jax.nn.gelu(jnp.einsum('bnd,bkdh->bknh', x, W1g) + b1g[:, :, None, :])
        eo = jnp.einsum('bknh,bkhd->bknd', h, W2g) + b2g[:, :, None, :]
        expert_out = jnp.einsum('bk,bknd->bnd', gate_w, eo)
        a = jnp.clip(alpha, 0.1, 1.0)
        return a * main + (1.0 - a) * expert_out
    x = L0_attn_x
    x = x + _L0_attn_ref(_layernorm(x, axis=-1), L0_attn_qkv_w, L0_attn_qkv_b, L0_attn_proj_w, L0_attn_proj_b, L0_attn_norm1_g, L0_attn_norm1_b, L0_attn_norm2_g, L0_attn_norm2_b, L0_attn_fc1_w, L0_attn_fc1_b, L0_attn_fc2_w, L0_attn_fc2_b)
    x = x + _L0_ffn_ref(_layernorm(x, axis=-1), L0_ffn_alpha, L0_ffn_w_gate, L0_ffn_b_gate, L0_ffn_W1m, L0_ffn_b1m, L0_ffn_W2m, L0_ffn_b2m, L0_ffn_W1e, L0_ffn_b1e, L0_ffn_W2e, L0_ffn_b2e)
    return x

_drawn_inputs = setup_inputs


def setup_inputs(seed=0):
    import zlib

    import numpy as np

    out = dict(_drawn_inputs(seed))
    spreads = {'L0_attn_norm1_g': (1.0, 0.6),
     'L0_attn_norm1_b': (0.0, 0.463),
     'L0_attn_norm2_g': (1.0, 0.6),
     'L0_attn_norm2_b': (0.0, 0.72),
     'L0_ffn_b_gate': (0.0, 0.8),
     'L0_ffn_b1m': (0.0, 0.509),
     'L0_ffn_b2m': (0.0, 0.1),
     'L0_ffn_b1e': (0.0, 0.8),
     'L0_ffn_b2e': (0.0, 2.0)}
    factors = {'L0_attn_qkv_b': 4.688,
     'L0_attn_proj_b': 3.091,
     'L0_attn_fc1_b': 8.0,
     'L0_attn_fc2_b': 6.474,
     'L0_ffn_w_gate': 8.0,
     'L0_ffn_W1e': 8.0,
     'L0_ffn_W2e': 8.0}
    for name, (base, spread) in spreads.items():
        noise = np.random.default_rng([zlib.crc32(name.encode()), seed]).standard_normal(out[name].shape)
        drawn = base * np.exp(spread * noise) if base else spread * noise
        out[name] = jnp.asarray(drawn.astype(out[name].dtype))
    for name, factor in factors.items():
        out[name] = (out[name] * factor).astype(out[name].dtype)
    return out
```

```python
from contextlib import ExitStack

import concourse.bass as bass
from concourse import mybir

P = 128
EPS = 1e-5
N_POOL = 23


class Plan:

    def __init__(self):
        self.ops, self.count, self.per, self.stage, self.final = [], {}, {}, None, {}

    def op(self, engine, kind, index, make, waits=(), dma=False, apart=False):
        if kind is not None:
            self.per[kind] = self.per.get(kind, 0) + (16 if dma else 1)
            assert (kind, index) not in self.count, (kind, index)
            self.count[(kind, index)] = self.per[kind]
        self.ops.append((self.stage, engine, kind, make, list(waits), 16 if dma else 1, apart))

    def emit(self, name, engine, sems, row_of, last=False):
        for stage, eng, kind, make, waits, amount, apart in self.ops:
            if eng != name or stage not in row_of:
                continue
            row = row_of[stage]
            least = {}
            for w in waits:
                key, back = w if isinstance(w[1], Back) else (w, Back(0))
                if back.runs < 0 and last:
                    continue
                for k in self.final[key[1]] if key[0] == "bank" else [key]:
                    at = (1 - back.runs) * self.per[k[0]] + self.count[k]
                    least[k[0]] = max(at, least.get(k[0], at))
            for k, at in least.items():
                engine.wait_ge(sems[k], row * self.per[k] + at)
            if apart:
                engine.sem_inc(self.idle, 1)
            made = make(engine, row)
            if kind is not None:
                made.then_inc(sems[kind], amount)


class Back:
    def __init__(self, runs):
        self.runs = runs


def before(kind, index):
    return ((kind, index), Back(1))


def beside(kind, index):
    return ((kind, index), Back(-1))


def build(nc, x, qkv_w, qkv_b, proj_w, proj_b, g1, b1, g2, b2, fc1_w, fc1_b, fc2_w, fc2_b,
          alpha, w_gate, b_gate, W1m, b1m, W2m, b2m, W1e, b1e, W2e, b2e, out):
    f32, f32r, u32 = mybir.dt.float32, mybir.dt.float32r, mybir.dt.uint32
    ALU, ACT, AX = mybir.AluOpType, mybir.ActivationFunctionType, mybir.AxisListType

    ROWS, T, D = x.shape
    HID = fc1_w.shape[1]
    E = w_gate.shape[1]
    KD, KH, NT = D // P, HID // P, T // P
    HD, RAD = 16, 7
    HS = 4
    QB = P // HS
    NB = T // QB
    KW = 48
    G = 2
    UB = NB // 2
    NP_ = UB // 2
    LEFT = 8
    ZW = LEFT + T + 26
    NCH = 3 * KH
    NX = 2 * KH
    RING = 4

    with ExitStack() as ctx:
        def sb(name, shape, dt=f32):
            return ctx.enter_context(nc.sbuf_tensor(name, shape, dt))

        def pair(name, shape):
            return [sb(f"{name}_hi", shape, f32r), sb(f"{name}_lo", shape, f32r)]
        wqkv = pair("wqkv", [P, KD, 3 * D])
        wproj = pair("wproj", [P, KD, D])
        wf1 = pair("wf1", [P, KD, HID])
        wf2 = pair("wf2", [P, KH, D])
        wm1 = pair("wm1", [P, KD, HID])
        wm2 = pair("wm2", [P, KH, D])
        CW = KD * P + D
        raw = sb("raw", [P, RING, CW])
        wx = pair("wx", [P, RING, CW])
        xin = sb("xin", [P, NT, D])
        y = sb("y", [P, NT, D])
        sx = sb("sx", [P, NT, D])
        acc = sb("acc", [P, NT, D])
        tm = sb("tm", [P, NT, D])
        zT = pair("zT", [P, KD, ZW])
        z3 = pair("z3", [P, KD, T])
        zf = sb("zf", [P, T])
        kT = sb("kT", [P, ZW])
        qm = sb("qm", [P, 2, UB, HS * QB])
        kb = sb("kb", [P, 2, UB, G * KW])
        vb = sb("vb", [P, NB // 2, KD * G, P])
        pr = sb("pr", [P, 2, 2, G, 4, 64])
        pT = sb("pT", [P, G, NP_, P])
        smax = sb("smax", [P, 2, UB * G])
        ssum = sb("ssum", [P, 2, UB * G])
        rinv = sb("rinv", [P, 4, 2, G, 4])
        hf = sb("hf", [P, 2, T])
        hr = pair("hr", [P, 2, T])
        ident = sb("ident", [P, P])
        band = sb("band", [P, KW])
        hmask = sb("hmask", [P, HS])
        ones = sb("ones", [1, P])
        keep = sb("keep", [P, 3])
        bv = sb("bv", [P, D])
        bproj = sb("bproj", [P, D])
        bfc2 = sb("bfc2", [P, D])
        b2all = sb("b2all", [E + 1, D])
        NSM = E * KH + 2 * KH + 2 * KD + 4 * KD
        small = sb("small", [NSM, P])
        smallT = sb("smallT", [P, NSM])
        wg = sb("wg", [P, KD, E])
        bg = sb("bg", [1, E])
        iota = sb("iota", [1, E])
        mhalf = sb("mhalf", [P, NT])
        st = sb("st", [P, NT, 6])
        mv = sb("mv", [P, 3, NT, 2])
        rs = sb("rs", [P, 6, NT])
        msum = sb("msum", [P, KD])
        lg = sb("lg", [1, E])
        m8 = sb("m8", [1, 8])
        idx = sb("idx", [1, 8], u32)
        idf = sb("idf", [1, 2])
        tw = sb("tw", [1, 4])
        al = sb("al", [1, 2])
        NR = 3 * E + 3
        rrow = sb("rrow", [1, NR])
        bc = sb("bc", [P, NR])
        cb = sb("cb", [E + 1, P])
        b1x = sb("b1x", [P, 2, KH])
        b1t = sb("b1t", [P, KH, E])

        psB = ctx.enter_context(nc.psum_tensor("psB", [P, 4, 512], f32))
        psA = ctx.enter_context(nc.psum_tensor("psA", [P, 4, 512], f32))

        oE, oM = 0, E * KH
        oF = oM + KH
        oQK = oF + KH
        oG1 = oQK + 2 * KD
        oB1, oG2, oB2 = oG1 + KD, oG1 + 2 * KD, oG1 + 3 * KD

        p = Plan()
        op = p.op

        def three(eng, dst, a, b, start, stop):
            for n, (u, v) in enumerate(((0, 0), (0, 1), (1, 0))):
                last = eng.matmul(dst, a[u], b[v], start=start and n == 0, stop=stop and n == 2)
            return last

        freed = {b: None for b in range(4)}

        def use(bank, readers):
            freed[bank] = readers

        def bankwait(bank):
            return [(("bank", bank), Back(1))] if freed[bank] is None else list(freed[bank])

        def ffn_weights(n):
            s, e, m = n % RING, n // KH, n % KH

            def load1(sp, row, s=s, e=e, m=m):
                ex = regs[e]
                return sp.dma_start(raw[:, s, 0:KD * P].rearrange("p (k n) -> p k n", k=KD),
                                    W1e[bass.ds(ex, 1), :, m * P:(m + 1) * P].rearrange("a (k p) n -> p (a k) n", p=P))

            def load2(sp, row, s=s, e=e, m=m):
                ex = regs[e]
                return sp.dma_start(raw[:, s, KD * P:], W2e[bass.ds(ex, 1), m * P:(m + 1) * P, :].rearrange("a p n -> p (a n)"))
            free = [("w_hi", n - RING), ("w_lo", n - RING)] if n >= RING else [before("w_hi", NX - RING + n), before("w_lo", NX - RING + n)]
            op("sp", f"raw{s}", (n, 0), load1, free, dma=True)
            op("sp", f"raw{s}", (n, 1), load2, dma=True)

        def ffn_split(n):
            s = n % RING
            free = ("down", KH + n - RING) if n >= RING else before("down", NCH - RING + n)
            op("act", "w_hi", n, lambda a, r, s=s: a.activation(wx[0][:, s, :], raw[:, s, :], ACT.Copy),
               [(f"raw{s}", (n, 1)), free])
            op("dve", "w_lo", n, lambda v, r, s=s: v.tensor_tensor(wx[1][:, s, :], raw[:, s, :], wx[0][:, s, :].bitcast(f32), ALU.subtract),
               [("w_hi", n)])

        def chunk_weights(m):
            if m < KH:
                return ([[w[:, k, m * P:(m + 1) * P] for w in wm1] for k in range(KD)], [w[:, m, :] for w in wm2])
            s = (m - KH) % RING
            return ([[w[:, s, k * P:(k + 1) * P] for w in wx] for k in range(KD)], [w[:, s, KD * P:] for w in wx])

        def h_split(kinds, m, pos, up_key, src, func, bias, h_free, t_free):
            op("act", kinds[0], m, lambda a, r: a.activation(hf[:, pos, :], src, func, bias=bias), [up_key] + t_free)
            op("act", kinds[1], m, lambda a, r: a.activation(hr[0][:, pos, :], hf[:, pos, :], ACT.Copy),
               [(kinds[0], m)] + h_free)
            op("dve", kinds[2], m, lambda v, r: v.tensor_tensor(hr[1][:, pos, :], hf[:, pos, :], hr[0][:, pos, :].bitcast(f32), ALU.subtract),
               [(kinds[1], m)])

        def ffn_up(m):
            w1, _ = chunk_weights(m)
            waits = [("z3_lo", 1)] if m == 0 else []
            if m >= KH:
                waits += [("w_lo", m - KH)]
            waits += [("gelu", m - 2)] if m >= 2 else [before("gelu", NCH - 2 + m)]

            def mm(pe, r, m=m):
                for k in range(KD):
                    last = three(pe, psB[:, m % 2, :], w1[k], [z[:, k, :] for z in z3], k == 0, k == KD - 1)
                return last
            op("pe", "up", m, mm, waits)

        SPLIT = 19
        order = [("f", m) for m in range(SPLIT)] + [("m", m) for m in range(KH)] + [("f", m) for m in range(SPLIT, NCH)]

        def ring_free(q):
            me = order[q][0]
            prev, m = order[q - 2]
            if me == "f" and prev == "f":
                return ([("down", m)], [("h_lo", m)]) if q >= 2 else ([before("down", m)], [before("h_lo", m)])
            if me == "m" and prev == "m":
                return [("mdown", m)], [("mh_lo", m)]
            if me == "m":
                return [before("down", m)], [before("h_lo", m)]
            own = order[q - 2 - KH][1]
            return [beside("mdown", m), ("down", own)], [beside("mh_lo", m), ("h_lo", own)]

        def ffn_hidden(m, q):
            if m < KH:
                bias = smallT[:, oM + m:oM + m + 1]
            else:
                bias = b1x[:, (m - KH) // KH, m % KH:m % KH + 1]
            h_free, t_free = ring_free(q)
            h_split(("gelu", "h_hi", "h_lo"), m, q % 2, ("up", m), psB[:, m % 2, :], ACT.Gelu_apprx_tanh, bias,
                    h_free, t_free + ([("b1x", 1)] if m == KH else []))

        def ffn_down(m, q):
            _, w2 = chunk_weights(m)
            f, j = divmod(m, KH)
            waits = [("h_lo", m)]
            if j == 0:
                waits += [("acc", (f - 1, 1))] if f else [before("acc", (2, 1))]

            def mm(pe, r, j=j, m=m):
                for i in range(NT):
                    a = [h[:, q % 2, i * P:(i + 1) * P] for h in hr]
                    last = three(pe, psB[:, 2 + i // 2, (i % 2) * D:(i % 2 + 1) * D], a, w2,
                                 j == 0 and i % 2 == 0, j == KH - 1 and i % 2 == 1)
                return last
            op("pe", "down", m, mm, waits)
            if j == KH - 1:
                for h in range(2):
                    waits = [("down", m)] + ([("acc", (f - 1, h))] if f else [("acc0", 0)])
                    c = bc[:, 3 * E + f:3 * E + f + 1]
                    sl = acc[:, 2 * h:2 * h + 2, :].rearrange("p i n -> p (i n)")
                    op("dve", "acc", (f, h), lambda v, r, h=h, c=c, sl=sl: v.scalar_tensor_tensor(
                        sl, psB[:, 2 + h, :], c, sl, ALU.mult, ALU.add), waits)

        regs = {}

        def route_load():
            def load(sp, row):
                for e in range(2):
                    regs[e] = sp.value_load(idx[0:1, e:e + 1], min_val=0, max_val=E - 1)
            op("sp", None, None, lambda sp, row: load(sp, row), [("idx", 0)], apart=True)

        def route_bcast():
            b = 0
            def mm(pe, r):
                pe.matmul(psA[:, b, 0:NR], ones[:, :], rrow[:, :], start=True, stop=True)
                return pe.matmul(psA[0:E + 1, b, 256:256 + P], rrow[:, 2 * E:3 * E + 1], ones[:, :], start=True, stop=True)
            op("pe", "route1", 0, mm, [("rrow", 6), ("bank", b)])
            op("dve", "cb", 0, lambda v, r: v.tensor_copy(cb[:, :], psA[0:E + 1, b, 256:256 + P]),
               [("route1", 0), before("route2", 0)])
            op("dve", "bc", 0, lambda v, r: v.tensor_copy(bc[:, :], psA[:, b, 0:NR]), [before("acc", (2, 1)), before("b1x", 1)])
            use(b, [before("bc", 0)])
            for k in range(2):
                op("dve", "b1t", k, lambda v, r, k=k: v.tensor_tensor(
                    b1t[:, :, :], smallT[:, oE:oE + E * KH].rearrange("p (e c) -> p c e", e=E),
                    bc[:, k * E:(k + 1) * E].unsqueeze(1).to_broadcast([P, KH, E]), ALU.mult),
                   [("bc", 0)] + ([("b1x", 0)] if k else []))
                op("dve", "b1x", k, lambda v, r, k=k: v.tensor_reduce(b1x[:, k, :], b1t[:, :, :], AX.X, ALU.add),
                   [("b1t", k), before("gelu", NCH - 1)])

        def route_bias():
            b = 1
            op("pe", "route2", 0, lambda pe, r: pe.matmul(psA[:, b, 0:D], cb[:, :], b2all[:, :], start=True, stop=True),
               [("cb", 0), ("bank", b)])
            op("dve", "acc0", 0, lambda v, r: v.tensor_tensor(
                acc[:, :, :], sx[:, :, :], psA[:, b, 0:D].unsqueeze(1).to_broadcast([P, NT, D]), ALU.add),
               [("route2", 0), before("store", 0), ("x2", 1)])
            use(b, [before("acc0", 0)])

        def stats(n, src, ready):
            for i in range(NT):
                op("dve", "st", (n, i), lambda v, r, i=i: v.bn_stats(st[:, i, :], src[:, i, :]),
                   (ready[i] if i < len(ready) else []) + ([("mv", (n - 1, i))] if n else [before("mv", (2, i))]))
                op("dve", "mv", (n, i), lambda v, r, i=i, n=n: v.bn_aggr(mv[:, n, i, :], st[:, i, :]),
                   [("st", (n, i))] + ([before("rp", (6, 8, 10)[n])] if i == 0 else []), apart=True)

        rp = [0]

        def pool_small(dst, a, b_, o, extra=()):
            n = rp[0]
            rp[0] += 1
            op("pool", "rp", n, lambda g, r: g.tensor_tensor(dst, a, b_, o),
               ([("rp", n - 1)] if n else []) + list(extra))

        def rstd(n, last_reader):
            var = mv[:, n, :, 1]
            pool_small(rs[:, 2 * n, :], var, epst[:, :], ALU.add, [("mv", (n, NT - 1))] + last_reader)
            pool_small(rs[:, 2 * n + 1, :], rs[:, 2 * n, :], mhalf[:, :], ALU.pow)

        epst = sb("epst", [P, NT])
        rn = sb("rn", [P, 3, NT])

        def norm1_stats():
            stats(0, xin, [[before("xload", 0)]])
            rstd(0, [before("y", NT - 1)])
            r0, v0 = rs[:, 1, :], mv[:, 0, :, 1]
            pool_small(rn[:, 0, :], v0, r0, ALU.mult)
            pool_small(rn[:, 0, :], rn[:, 0, :], r0, ALU.mult)
            pool_small(rn[:, 0, :], rn[:, 0, :], epst[:, :], ALU.add)
            pool_small(rn[:, 1, :], rn[:, 0, :], mhalf[:, :], ALU.pow)
            pool_small(rn[:, 2, :], rn[:, 1, :], r0, ALU.mult)

        def norm1_apply():
            for i in range(NT):
                op("dve", "z", (0, i), lambda v, r, i=i: v.tensor_scalar(
                    tm[:, i, :], xin[:, i, :], mv[:, 0, i, 0:1], rn[:, 2, i:i + 1], ALU.subtract, ALU.mult),
                   [("rp", 6), before("tr3", 1)] if i == 0 else [])
            for i in range(NT):
                op("dve", "y", i, lambda v, r, i=i: v.tensor_scalar(
                    y[:, i, :], xin[:, i, :], mv[:, 0, i, 0:1], rs[:, 1, i:i + 1], ALU.subtract, ALU.mult),
                   [before("sx", 0)] if i == 0 else [])
            op("pool", "yb", 0, lambda g, r: g.tensor_tensor(
                y[:, :, :], y[:, :, :], bproj[:, :].unsqueeze(1).to_broadcast([P, NT, D]), ALU.add), [("y", NT - 1)])

        def transposes(kind, c, bank, waits):
            def mm(pe, r):
                for i in range(NT):
                    last = pe.transpose(psA[:, bank, i * P:(i + 1) * P], tm[:, i, c * P:(c + 1) * P], ident[:, :])
                return last
            op("pe", kind, c, mm, waits + bankwait(bank))

        def split_T(kind, c, bank, src_key, gain, bias, dst, off, free, banks_reader):
            op("act", kind + "_f", c, lambda a, r: a.activation(zf[:, :], psA[:, bank, :], ACT.Identity, bias=bias, scale=gain),
               [src_key, banks_reader])
            use(bank, [(kind + "_f", c)])
            op("act", kind + "_hi", c, lambda a, r: a.activation(dst[0][:, c, off:off + T], zf[:, :], ACT.Copy),
               [(kind + "_f", c)] + free)
            op("dve", kind + "_lo", c, lambda v, r: v.tensor_tensor(
                dst[1][:, c, off:off + T], zf[:, :], dst[0][:, c, off:off + T].bitcast(f32), ALU.subtract),
               [(kind + "_hi", c)])

        def split_plain(kind, c, bank, src_key, dst, off, free, accum=None):
            op("act", kind + "_hi", c, lambda a, r: a.activation(dst[0][:, c, off:off + T], psA[:, bank, :], ACT.Identity, accum_out=accum)
               if accum is not None else a.activation(dst[0][:, c, off:off + T], psA[:, bank, :], ACT.Identity),
               [src_key] + free)
            op("dve", kind + "_lo", c, lambda v, r: v.tensor_tensor(
                dst[1][:, c, off:off + T], psA[:, bank, :], dst[0][:, c, off:off + T].bitcast(f32), ALU.subtract),
               [(kind + "_hi", c)])
            use(bank, [(kind + "_lo", c)])

        def tr1(c):
            transposes("tr1", c, 2 + c, [("z", (0, NT - 1))])
            zf_free = ("t1_lo", 0) if c else before("t2_lo", 1)
            split_T("t1", c, 2 + c, ("tr1", c), smallT[:, oG1 + c:oG1 + c + 1], smallT[:, oB1 + c:oB1 + c + 1],
                    zT, LEFT, [before("mup", KH - 1)], zf_free)

        def qk(c):
            for which, bank in ((1, 0), (0, 1)):
                col = which * D + c * P

                def mm(pe, r, bank=bank, col=col):
                    for k in range(KD):
                        last = three(pe, psA[:, bank, :], [w[:, k, col:col + P] for w in wqkv],
                                     [z[:, k, LEFT:LEFT + T] for z in zT], k == 0, k == KD - 1)
                    return last
                op("pe", "qk", (c, which), mm, [("t1_lo", 1)] + bankwait(bank))
                j = which * KD + c
                bias = smallT[:, oQK + j:oQK + j + 1]
                if which == 1:
                    op("act", "kT", c, lambda a, r, bank=bank, bias=bias: a.activation(
                        kT[:, LEFT:LEFT + T], psA[:, bank, :], ACT.Identity, bias=bias),
                       [("qk", (c, 1)), ("kb", (1, 1)) if c else before("kb", (3, 1))])
                    use(bank, [("kT", c)])
            for th in range(2):
                u = 2 * c + th
                for g in range(G):
                    rows = slice(64 * g, 64 * g + 64)
                    base = LEFT - RAD + th * UB * QB
                    win = bass.AP(kT[rows, base:base + 1].tensor, kT[rows, base:base + 1].offset,
                                  [kT[rows, base:base + 1].ap[0], [QB, UB], [1, KW]])
                    op("act", "kb", (u, g), lambda a, r, th=th, g=g, rows=rows, win=win: a.activation(
                        kb[rows, th, :, g * KW:(g + 1) * KW], win, ACT.Copy),
                       [("kT", c), ("score", (u - 2, 1)) if c else before("score", (u + 2, 1))])
                for s in range(HS):
                    op("dve", "qm", (u, s), lambda v, r, th=th, s=s, c=c: v.tensor_scalar(
                        qm[:, th, :, s * QB:(s + 1) * QB],
                        psA[:, 1, th * UB * QB:(th + 1) * UB * QB].rearrange("p (b q) -> p b q", q=QB),
                        smallT[:, oQK + c:oQK + c + 1], hmask[:, s:s + 1], ALU.add, ALU.mult),
                       [("qk", (c, 0)), ("score", (u - 2, 1)) if c else before("score", (u + 2, 1))])
            use(1, [("qm", (2 * c + 1, HS - 1))])

        def values(n):
            bank = 2 + n % 2

            def mm(pe, r):
                for j in range(2):
                    base = LEFT - RAD + (4 * n + j) * QB
                    for k in range(KD):
                        last = three(pe, psA[:, bank, j * D:(j + 1) * D], [z[:, k, base:base + P] for z in zT],
                                     [w[:, k, 2 * D:] for w in wqkv], k == 0, k == KD - 1)
                return last
            op("pe", "val", n, mm, [("t1_lo", 1)] + bankwait(bank))
            for j in range(2):
                i = 2 * n + j
                kc = 0 if i == 0 else 2 if i == NB // 2 - 1 else 1
                for s in range(2):
                    rows = slice(64 * s, 64 * s + 64)
                    op("dve", "vb", (i, s), lambda v, r, i=i, j=j, s=s, rows=rows, kc=kc: v.scalar_tensor_tensor(
                        vb[rows, i, :, 64 * s:64 * s + 64], bv[rows, :].rearrange("p (g n) -> p g n", n=64),
                        keep[rows, kc:kc + 1], psA[rows, bank, j * D:(j + 1) * D].rearrange("p (g n) -> p g n", n=64),
                        ALU.mult, ALU.add),
                       [("val", n), before("av", (3, 1))])
            use(bank, [("vb", (2 * n + 1, 1))])

        def place(j):
            return 2 * (j % 2) + j // 2

        def score(u, b0):
            th = u % 2
            for h in range(2):
                bank = b0 + h

                def mm(pe, r, h=h, bank=bank):
                    for j in range(4):
                        b = 4 * h + j
                        dst = psA[:, bank, 0:4 * G * KW].rearrange("p (g b k) -> p g b k", g=G, k=KW)[:, :, place(j), :]
                        last = pe.matmul(dst, qm[:, th, b, :], kb[:, th, b, :].rearrange("p (g k) -> p g k", g=G),
                                         start=True, stop=True)
                    return last
                op("pe", "score", (u, h), mm, [("qm", (u, HS - 1)), ("kb", (u, 1))] + bankwait(bank))
                op("dve", "masked", (u, h), lambda v, r, h=h, bank=bank: v.scalar_tensor_tensor(
                    pr[:, th, h, :, :, 0:KW].rearrange("p g b k -> p (g b) k"),
                    psA[:, bank, 0:4 * G * KW].rearrange("p (n k) -> p n k", k=KW), HD ** -0.5,
                    band[:, :].unsqueeze(1).to_broadcast([P, 4 * G, KW]), ALU.mult, ALU.add),
                   [("score", (u, h)), ("trp", (u - 2, 1)) if u >= 2 else before("trp", (u + 2, 1))])
                use(bank, [("masked", (u, h))])

        def unit_scores(u):
            return pr[:, u % 2, :, :, :, 0:KW].rearrange("p t g b k -> p (t g b) k")

        def shift(u):
            th, s = u % 2, unit_scores(u)
            op("dve", "smax", u, lambda v, r: v.tensor_reduce(smax[:, th, :], s, AX.X, ALU.max), [("masked", (u, 1))])
            op("dve", "shift", u, lambda v, r: v.tensor_tensor(
                s, s, smax[:, th, :].unsqueeze(2).to_broadcast([P, UB * G, KW]), ALU.subtract), [("smax", u)])

        def exp(u):
            s = unit_scores(u)
            op("act", "exp", u, lambda a, r: a.activation(s, s, ACT.Exp), [("shift", u)])

        def sums(u):
            th, s = u % 2, unit_scores(u)
            op("dve", "ssum", u, lambda v, r: v.tensor_reduce(ssum[:, th, :], s, AX.X, ALU.add), [("exp", u)])
            op("dve", "rinv", u, lambda v, r: v.reciprocal(
                rinv[:, u, :, :, :].rearrange("p t g b -> p (t g b)"), ssum[:, th, :]), [("ssum", u)])

        def probT(u, b0):
            th = u % 2
            for g in range(G):
                bank = b0 + g

                def mm(pe, r, g=g, bank=bank):
                    for j in range(NP_):
                        last = pe.transpose(psA[:, bank, j * P:(j + 1) * P], pr[:, th, j // 2, g, 2 * (j % 2):2 * (j % 2) + 2, :].rearrange("p b k -> p (b k)"), ident[:, :])
                    return last
                op("pe", "trp", (u, g), mm, [("exp", u)] + bankwait(bank))
                op("act", "pT", (u, g), lambda a, r, g=g, bank=bank: a.activation(
                    pT[:, g, :, :].rearrange("p j q -> p (j q)"), psA[:, bank, :], ACT.Copy),
                   [("trp", (u, g)), ("av", (u - 1, g)) if u else before("av", (3, g))])
                use(bank, [("pT", (u, g))])

        def attend(u, b0):
            c, th = divmod(u, 2)
            for g in range(G):
                bank = b0 + g

                def mm(pe, r, g=g, bank=bank):
                    for j in range(NP_):
                        last = pe.matmul(psA[:, bank, j * P:(j + 1) * P], pT[:, g, j, :],
                                         vb[:, th * NP_ + j, c * G + g, :], start=True, stop=True)
                    return last
                op("pe", "av", (u, g), mm, [("pT", (u, g)), ("vb", (NB // 2 - 1, 1))] + bankwait(bank))
            for h in range(HS):
                for b in range(P // QB):
                    src = psA[QB * h:QB * h + QB, b0:b0 + 2, :].rearrange(
                        "p g (t j s n) -> p g t j s n", t=2, j=2, s=2)[:, :, :, b % 2, b // 2, HD * h:HD * h + HD]
                    f0 = c * P + HD * h
                    dst = tm[QB * b:QB * b + QB, 2 * th:2 * th + 2, c * P:(c + 1) * P].rearrange(
                        "p t (g n) -> p g t n", g=G)[:, :, :, HD * h:HD * h + HD]
                    w = rinv[QB * h:QB * h + QB, u, :, :, :].rearrange("p t g b -> p g t b")[:, :, :, place(b)]\
                        .unsqueeze(3).to_broadcast([QB, G, 2, HD])
                    op("dve", "att", (u, h, b), lambda v, r, src=src, dst=dst, w=w: v.tensor_tensor(dst, src, w, ALU.mult),
                       [("av", (u, 1)), ("rinv", u), ("tr1", 1)] if (h, b) == (0, 0) else [])
            for g in range(G):
                use(b0 + g, [("att", (u, HS - 1, P // QB - 1))])

        def attT(c, bank):
            transposes("trA", c, bank, [("att", (3, HS - 1, P // QB - 1))])
            split_plain("tA", c, bank, ("trA", c), zT, LEFT, [("val", NB // 4 - 1), ("qk", (1, 0))])

        def project(b0):
            for h in range(2):
                bank = b0 + h

                def mm(pe, r, h=h, bank=bank):
                    for j in range(2):
                        i = 2 * h + j
                        for k in range(KD):
                            last = three(pe, psA[:, bank, j * D:(j + 1) * D],
                                         [z[:, k, LEFT + i * P:LEFT + (i + 1) * P] for z in zT],
                                         [w[:, k, :] for w in wproj], k == 0, k == KD - 1)
                    return last
                op("pe", "proj", h, mm, [("tA_lo", 1)] + bankwait(bank))
                sl = y[:, 2 * h:2 * h + 2, :].rearrange("p i n -> p (i n)")
                op("dve", "x1", h, lambda v, r, bank=bank, sl=sl: v.tensor_tensor(sl, sl, psA[:, bank, :], ALU.add),
                   [("proj", h), ("yb", 0)])
                use(bank, [("x1", h)])

        def norm2_stats():
            stats(1, y, [[("x1", 0)], [], [("x1", 1)], []])
            rstd(1, [before("z", (1, NT - 1))])
            op("pool", "sx", 0, lambda g, r: g.tensor_tensor(sx[:, :, :], xin[:, :, :], y[:, :, :], ALU.add),
               [("x1", 1), before("acc0", 0)])
            op("pool", "sxb", 0, lambda g, r: g.tensor_tensor(
                sx[:, :, :], sx[:, :, :], bfc2[:, :].unsqueeze(1).to_broadcast([P, NT, D]), ALU.add), [("sx", 0)])

        def norm2_apply():
            for i in range(NT):
                op("dve", "z", (1, i), lambda v, r, i=i: v.tensor_scalar(
                    tm[:, i, :], y[:, i, :], mv[:, 1, i, 0:1], rs[:, 3, i:i + 1], ALU.subtract, ALU.mult),
                   [("rp", 8), ("trA", 1)] if i == 0 else [])

        def tr2(c, bank):
            transposes("tr2", c, bank, [("z", (1, NT - 1))])
            split_T("t2", c, bank, ("tr2", c), smallT[:, oG2 + c:oG2 + c + 1], smallT[:, oB2 + c:oB2 + c + 1],
                    zT, LEFT, [("proj", 1)], ("t2_lo", 0) if c else ("t1_lo", 1))

        def mlp_up(m):
            def mm(pe, r):
                for k in range(KD):
                    last = three(pe, psA[:, m % 2, :], [w[:, k, m * P:(m + 1) * P] for w in wf1],
                                 [z[:, k, LEFT:LEFT + T] for z in zT], k == 0, k == KD - 1)
                return last
            op("pe", "mup", m, mm, [("t2_lo", 1)] + bankwait(m % 2))
            use(m % 2, [("mgelu", m)])

        def mlp_hidden(m, q):
            h_free, t_free = ring_free(q)
            h_split(("mgelu", "mh_hi", "mh_lo"), m, q % 2, ("mup", m), psA[:, m % 2, :], ACT.Gelu,
                    smallT[:, oF + m:oF + m + 1], h_free, t_free)

        def mlp_down(m, q):
            def mm(pe, r):
                for i in range(NT):
                    a = [h[:, q % 2, i * P:(i + 1) * P] for h in hr]
                    last = three(pe, psA[:, 2 + i // 2, (i % 2) * D:(i % 2 + 1) * D], a, [w[:, m, :] for w in wf2],
                                 m == 0 and i % 2 == 0, m == KH - 1 and i % 2 == 1)
                return last
            op("pe", "mdown", m, mm, [("mh_lo", m)] + (bankwait(2) + bankwait(3) if m == 0 else []))
            if m == KH - 1:
                for h in range(2):
                    sl = sx[:, 2 * h:2 * h + 2, :].rearrange("p i n -> p (i n)")
                    op("dve", "x2", h, lambda v, r, h=h, sl=sl: v.tensor_tensor(sl, sl, psA[:, 2 + h, :], ALU.add),
                       [("mdown", KH - 1), ("sxb", 0)])
                    use(2 + h, [("x2", h)])

        def norm3_stats():
            stats(2, sx, [[("x2", 0)], [], [("x2", 1)], []])
            rstd(2, [before("z", (2, NT - 1))])

        def norm3_apply():
            for i in range(NT):
                op("dve", "z", (2, i), lambda v, r, i=i: v.tensor_scalar(
                    tm[:, i, :], sx[:, i, :], mv[:, 2, i, 0:1], rs[:, 5, i:i + 1], ALU.subtract, ALU.mult),
                   [("rp", 10), ("tr2", 1)] if i == 0 else [])

        def tr3(c, bank):
            transposes("tr3", c, bank, [("z", (2, NT - 1))])
            split_plain("z3", c, bank, ("tr3", c), z3, 0, [before("up", NCH - 1), before("router", 0)], msum[:, c:c + 1])

        def router(bank):
            def mm(pe, r):
                for k in range(KD):
                    last = pe.matmul(psA[0:1, bank, 0:E], msum[:, k:k + 1], wg[:, k, :], start=k == 0, stop=k == KD - 1)
                return last
            op("pe", "router", 0, mm, [("z3_hi", 1)] + bankwait(bank))
            use(bank, [("lg", 0)])
            op("dve", "lg", 0, lambda v, r: v.scalar_tensor_tensor(
                lg[:, :], psA[0:1, bank, 0:E], 1.0 / T, bg[:, :], ALU.mult, ALU.add), [("router", 0)])
            op("dve", "m8", 0, lambda v, r: v.max(m8[:, :], lg[:, :]), [("lg", 0)], apart=True)
            op("dve", "idx", 0, lambda v, r: v.max_index(idx[:, :], m8[:, :], lg[:, :]), [("m8", 0), before(f"raw{RING - 1}", (NX - 1, 1))], apart=True)
            op("dve", "tw", 0, lambda v, r: v.tensor_tensor(tw[:, 0:1], m8[:, 0:1], m8[:, 1:2], ALU.subtract), [("m8", 0)])
            op("act", "tanh", 0, lambda a, r: a.activation(tw[:, 1:2], tw[:, 0:1], ACT.Tanh, scale=0.5), [("tw", 0)])
            op("dve", "idf", 0, lambda v, r: v.tensor_copy(idf[:, :], idx[:, 0:2]), [("idx", 0)])
            for k in range(2):
                op("dve", "rrow", k, lambda v, r, k=k: v.tensor_scalar(
                    rrow[:, k * E:(k + 1) * E], iota[:, :], idf[:, k:k + 1], None, ALU.is_equal),
                   [("idf", 0), before("route1", 0)])
            for k in range(2):
                op("dve", "rrow", 2 + k, lambda v, r, k=k: v.tensor_scalar(
                    tw[:, 2 + k:3 + k], tw[:, 1:2], 0.5 - k, 0.5, ALU.mult, ALU.add), [("tanh", 0)])
            op("dve", "rrow", 4, lambda v, r: v.tensor_scalar(
                rrow[:, 3 * E + 1:3 * E + 3], tw[:, 2:4], al[:, 1:2], None, ALU.mult), [("rrow", 3)])
            op("dve", "rrow", 5, lambda v, r: v.tensor_scalar(
                rrow[:, 2 * E:3 * E], rrow[:, 0:E], rrow[:, 3 * E + 1:3 * E + 2], None, ALU.mult), [("rrow", 4)])
            op("dve", "rrow", 6, lambda v, r: v.scalar_tensor_tensor(
                rrow[:, 2 * E:3 * E], rrow[:, E:2 * E], rrow[:, 3 * E + 2:3 * E + 3], rrow[:, 2 * E:3 * E], ALU.mult, ALU.add),
               [("rrow", 5)])

        pieces = []
        qkv_v = qkv_w.rearrange("(k p) n -> p k n", p=P)
        for k in range(KD):
            for h in range(2):
                c = slice(h * 3 * D // 2, (h + 1) * 3 * D // 2)
                pieces.append((qkv_v[:, k, c], [w[:, k, c] for w in wqkv], None))
        pieces.append((proj_w.rearrange("(k p) n -> p k n", p=P), [w[:, :, :] for w in wproj], KD))

        def first_layer(w, dst):
            v = w.rearrange("(k p) n -> p k n", p=P)
            for k in range(KD):
                for h in range(HID // CW):
                    c = slice(h * CW, (h + 1) * CW)
                    pieces.append((v[:, k, c], [d[:, k, c] for d in dst], None))

        def second_layer(w, dst):
            v = w.rearrange("(m p) n -> p m n", p=P)
            n = CW // D
            for m in range(0, KH, n):
                pieces.append((v[:, m:m + n, :], [d[:, m:m + n, :] for d in dst], n))
        first_layer(fc1_w, wf1)
        second_layer(fc2_w, wf2)
        first_layer(W1m, wm1)
        second_layer(W2m, wm2)

        def raw_piece(n):
            _, dst, inner = pieces[n]
            width = 1
            for d in dst[0].shape[1:]:
                width *= d
            v = raw[:, n % RING, 0:width]
            return v.rearrange("p (k n) -> p k n", k=inner) if inner else v

        start_steps = []

        def weights(a, b):
            def f():
                for n in range(a, b):
                    s = n % RING
                    _, dst, _ = pieces[n]
                    op("sp", f"praw{s}", n, lambda sp, r, n=n: sp.dma_start(raw_piece(n), pieces[n][0]),
                       [("p_lo", n - RING)] if n >= RING else [], dma=True)
                    op("act", "p_hi", n, lambda a, r, n=n, dst=dst: a.activation(dst[0], raw_piece(n), ACT.Copy), [(f"praw{s}", n)])
                    op("dve", "p_lo", n, lambda v, r, n=n, dst=dst: v.tensor_tensor(
                        dst[1], raw_piece(n), dst[0].bitcast(f32), ALU.subtract), [("p_hi", n)])
            start_steps.append(f)
            return f

        def ready(n):
            def f():
                op("pe", None, None, lambda pe, r: None, [("p_lo", n - 1)])
            start_steps.append(f)
            return f

        def both(f, *args):
            return lambda: [f(*a) for a in args]

        steps = {
            -1: [route_load, weights(0, 4), norm1_stats],
            1: [route_bcast],
            2: [norm1_apply, route_bias],
            3: [both(tr1, (0,), (1,)), weights(4, 6)],
            4: [ready(4), both(qk, (0,))],
            5: [both(values, (0,), (1,)), weights(6, 8)],
            6: [both(score, (0, 0)), both(values, (2,)), both(shift, (0,))],
            7: [both(score, (1, 0)), both(values, (3,)), both(shift, (1,)), weights(8, 10)],
            8: [both(exp, (0,), (1,)), both(qk, (1,)), both(sums, (0,))],
            9: [both(probT, (0, 0)), both(sums, (1,))],
            10: [both(attend, (0, 2)), both(probT, (1, 0)), both(score, (2, 0)), both(shift, (2,)), weights(10, 12)],
            11: [both(attend, (1, 2)), both(score, (3, 0)), both(shift, (3,)), both(exp, (2,), (3,)), both(sums, (2,))],
            12: [both(probT, (2, 0)), both(sums, (3,)), weights(12, 13)],
            13: [both(attend, (2, 2)), both(probT, (3, 0))],
            14: [both(attend, (3, 2))],
            15: [both(attT, (0, 0), (1, 1)), ready(5), both(project, (2,)), norm2_stats],
            17: [norm2_apply],
            18: [both(tr2, (0, 0), (1, 1)), ready(13)],
            22: [weights(13, 17)],
            24: [weights(17, 21)],
            28: [norm3_stats],
            30: [norm3_apply],
            31: [both(tr3, (0, 0), (1, 1))],
            32: [both(router, (2,))],
        }
        route_steps = (route_load, route_bcast, route_bias)

        def run_steps(s):
            for f in steps.get(s, ()):
                p.stage = "route" if f in route_steps else "start" if f in start_steps else "attn"
                f()

        run_steps(-1)
        loads = 0
        for q in range(len(order) + 2):
            if q < len(order):
                kind, m = order[q]
                if kind == "f":
                    p.stage = "ffn"
                    while loads < NX and loads < m + RING + 1:
                        ffn_weights(loads)
                        loads += 1
                    if 3 <= m < 3 + RING:
                        ffn_split(m - 3)
                    if RING <= m - KH + 1 < NX:
                        ffn_split(m - KH + 1)
                    ffn_up(m)
                else:
                    p.stage = "attn"
                    mlp_up(m)
            if q >= 2:
                kind, m = order[q - 2]
                p.stage = "ffn" if kind == "f" else "attn"
                (ffn_down if kind == "f" else mlp_down)(m, q - 2)
            if q < len(order):
                kind, m = order[q]
                p.stage = "ffn" if kind == "f" else "attn"
                (ffn_hidden if kind == "f" else mlp_hidden)(m, q)
            if q == 26:
                p.stage = "attn"
                op("sp", "xload", 0, lambda sp, r: sp.dma_start(
                    xin[:, :, :], x[bass.ds((r + 1) % ROWS, 1), :, :].rearrange("a (i p) n -> p (a i) n", p=P)),
                   [("sx", 0)], dma=True)
            run_steps(q)
        p.stage = "start"
        for e in ("pe", "sp"):
            op(e, None, None, lambda eng, r: None, [("p_lo", len(pieces) - 1)])
        p.stage = "ffn"
        op("sp", "store", 0, lambda sp, r: sp.dma_start(
            out[bass.ds(r, 1), :, :].rearrange("a (i p) n -> p (a i) n", p=P), acc[:, :, :]), [("acc", (2, 1))], dma=True)
        p.final = freed

        sems = {k: ctx.enter_context(nc.semaphore(f"s_{k}")) for k in p.per}
        start = {k: ctx.enter_context(nc.semaphore(f"c_{k}")) for k in
                 ("x", "small", "rows", "pool", "dve", "smallT", "smallP")}

        p.idle = ctx.enter_context(nc.semaphore("c_idle"))

        def prime(engine, name):
            for k in p.per:
                if any(o[1] == name and o[2] == k for o in p.ops):
                    engine.sem_inc(sems[k], p.per[k])

        def runs(engine, name):
            p.emit(name, engine, sems, {"start": 0, "attn": 0})
            with engine.Fori(0, ROWS - 1) as i:
                p.emit(name, engine, sems, {"route": i, "ffn": i, "attn": i + 1})
            p.emit(name, engine, sems, {"route": ROWS - 1, "ffn": ROWS - 1}, last=True)

        block = ctx.enter_context(nc.Block())

        @block.sync
        def _(sp):
            prime(sp, "sp")

            sp.dma_start(xin[:, :, :], x[0, :, :].rearrange("(i p) n -> p i n", p=P)).then_inc(start["x"], 16)
            rows = [(b1e.rearrange("e (c p) -> (e c) p", p=P), oE, E * KH), (b1m.rearrange("(c p) -> c p", p=P), oM, KH),
                    (fc1_b.rearrange("(c p) -> c p", p=P), oF, KH), (qkv_b.rearrange("(c p) -> c p", p=P)[0:2 * KD, :], oQK, 2 * KD),
                    (g1.rearrange("(c p) -> c p", p=P), oG1, KD), (b1.rearrange("(c p) -> c p", p=P), oB1, KD),
                    (g2.rearrange("(c p) -> c p", p=P), oG2, KD), (b2.rearrange("(c p) -> c p", p=P), oB2, KD)]
            for src, at, n in rows:
                sp.dma_start(small[at:at + n, :], src).then_inc(start["small"], 16)
            one = lambda a: a.rearrange("(o n) -> o n", o=1)
            for src, dst in ((qkv_b[2 * D:3 * D], bv), (proj_b, bproj), (fc2_b, bfc2)):
                sp.dma_start(dst[:, :], one(src).to_broadcast([P, D])).then_inc(start["rows"], 16)
            sp.dma_start(b2all[0:E, :], b2e).then_inc(start["rows"], 16)
            sp.dma_start(b2all[E:E + 1, :], one(b2m)).then_inc(start["rows"], 16)
            sp.dma_start(wg[:, :, :], w_gate.rearrange("(k p) e -> p k e", p=P)).then_inc(start["rows"], 16)
            sp.dma_start(bg[:, :], one(b_gate)).then_inc(start["rows"], 16)
            sp.dma_start(al[:, 0:1], one(alpha)).then_inc(start["rows"], 16)
            sp.wait_ge(start["smallT"], 1)
            runs(sp, "sp")
            sp.wait_ge(sems["store"], (ROWS + 1) * p.per["store"])

        @block.gpsimd
        def _(g):
            prime(g, "pool")
            n = 0

            def link(ins):
                nonlocal n
                n += 1
                ins.then_inc(start["pool"], 1)
                g.wait_ge(start["pool"], n)
            link(g.memset(ident[:, :], 0.0))
            link(g.affine_select(out=ident[:, :], in_=ident[:, :], compare_op=ALU.not_equal, fill=1.0, base=0,
                                 pattern=[[-1, P]], channel_multiplier=1))
            link(g.memset(epst[:, :], EPS))
            link(g.memset(mhalf[:, :], -0.5))
            link(g.memset(band[:, :], 0.0))
            for h in range(HS):
                v = band[QB * h:QB * h + QB, :]
                link(g.affine_select(out=v, in_=v, compare_op=ALU.is_ge, fill=-1e30, base=0, pattern=[[1, KW]], channel_multiplier=-1))
                link(g.affine_select(out=v, in_=v, compare_op=ALU.is_ge, fill=-1e30, base=2 * RAD, pattern=[[-1, KW]], channel_multiplier=1))
            link(g.memset(hmask[:, :], 1.0))
            for h in range(2):
                v = hmask[64 * h:64 * h + 64, :]
                link(g.affine_select(out=v, in_=v, compare_op=ALU.is_ge, fill=0.0, base=0, pattern=[[-HD, HS]], channel_multiplier=1))
                link(g.affine_select(out=v, in_=v, compare_op=ALU.is_ge, fill=0.0, base=HD - 1, pattern=[[HD, HS]], channel_multiplier=-1))
            link(g.memset(keep[:, :], 1.0))
            link(g.affine_select(out=keep[:, 0:1], in_=keep[:, 0:1], compare_op=ALU.is_ge, fill=0.0, base=-RAD, pattern=[[0, 1]], channel_multiplier=1))
            link(g.affine_select(out=keep[:, 2:3], in_=keep[:, 2:3], compare_op=ALU.is_ge, fill=0.0, base=64 + QB + RAD - 1, pattern=[[0, 1]], channel_multiplier=-1))
            link(g.memset(ones[:, :], 1.0))
            link(g.iota(iota[:, :], pattern=[[1, E]], base=0, channel_multiplier=0, allow_small_or_imprecise_dtypes=True))
            g.wait_ge(start["rows"], 16 * 8)
            runs(g, "pool")
            assert n == N_POOL, n

        @block.vector
        def _(v):
            prime(v, "dve")
            zeros = [kT[:, 0:LEFT], kT[:, LEFT + T:ZW], kb[:, :, :, :], pr[:, :, :, :, :, :], vb[:, :, :, :]]
            for z in zT:
                zeros += [z[:, :, 0:LEFT].bitcast(f32), z[:, :, LEFT + T:ZW].bitcast(f32)]
            for z in zeros:
                v.memset(z, 0.0).then_inc(start["dve"], 1)
            v.wait_ge(start["rows"], 16 * 8)
            v.tensor_scalar(rrow[:, 3 * E:3 * E + 1], al[:, 0:1], 0.1, 1.0, ALU.max, ALU.min).then_inc(start["dve"], 1)
            v.wait_ge(start["dve"], len(zeros) + 1)
            v.tensor_scalar(al[:, 1:2], rrow[:, 3 * E:3 * E + 1], -1.0, 1.0, ALU.mult, ALU.add).then_inc(start["dve"], 1)
            v.wait_ge(start["dve"], len(zeros) + 2)
            v.wait_ge(start["smallP"], 1)
            v.tensor_copy(smallT[:, :], psA[:, 0, 0:NSM]).then_inc(start["smallT"], 1)
            v.wait_ge(start["smallT"], 1)
            v.wait_ge(start["x"], 16)
            v.wait_ge(start["pool"], N_POOL)
            runs(v, "dve")

        @block.scalar
        def _(a):
            prime(a, "act")
            a.wait_ge(start["smallT"], 1)
            a.wait_ge(start["dve"], len(zT) * 2 + 5)
            runs(a, "act")

        @block.tensor
        def _(pe):
            prime(pe, "pe")
            pe.wait_ge(start["small"], 16 * 8)
            pe.wait_ge(start["pool"], N_POOL)
            pe.transpose(psA[:, 0, 0:NSM], small[:, :], ident[0:NSM, 0:NSM]).then_inc(start["smallP"], 1)
            pe.wait_ge(start["smallT"], 1)
            pe.wait_ge(start["rows"], 16 * 8)
            runs(pe, "pe")


_INS = ['L0_attn_x', 'L0_attn_qkv_w', 'L0_attn_qkv_b', 'L0_attn_proj_w', 'L0_attn_proj_b', 'L0_attn_norm1_g',
        'L0_attn_norm1_b', 'L0_attn_norm2_g', 'L0_attn_norm2_b', 'L0_attn_fc1_w', 'L0_attn_fc1_b', 'L0_attn_fc2_w',
        'L0_attn_fc2_b', 'L0_ffn_alpha', 'L0_ffn_w_gate', 'L0_ffn_b_gate', 'L0_ffn_W1m', 'L0_ffn_b1m', 'L0_ffn_W2m',
        'L0_ffn_b2m', 'L0_ffn_W1e', 'L0_ffn_b1e', 'L0_ffn_W2e', 'L0_ffn_b2e']


def kernel(**inputs):
    import numpy as np
    import concourse.bacc as bacc
    from concourse.bass_utils import run_bass_kernel_spmd

    nc = bacc.Bacc("TRN2", target_bir_lowering=False, num_devices=1)
    arrays, args = {}, []
    for name in _INS:
        a = np.ascontiguousarray(inputs[name])
        if a.ndim == 0:
            a = a.reshape(1)
        arrays["in_" + name] = a
        args.append(nc.dram_tensor("in_" + name, a.shape, mybir.dt.from_np(a.dtype), kind="ExternalInput").ap())
    shape = arrays["in_L0_attn_x"].shape
    args.append(nc.dram_tensor("out_x", shape, mybir.dt.float32, kind="ExternalOutput").ap())
    build(nc, *args)
    r = run_bass_kernel_spmd(nc, [arrays], core_ids=[0])
    return r.results[0]["out_x"]
```

```python
from contextlib import ExitStack

import concourse.bass as bass
from concourse import mybir

P = 128
EPS = 1e-5
N_POOL = 25


class Plan:

    def __init__(self):
        self.ops, self.count, self.per, self.stage, self.final = [], {}, {}, None, {}

    def op(self, engine, kind, index, make, waits=(), dma=False, apart=False):
        if kind is not None:
            self.per[kind] = self.per.get(kind, 0) + (16 if dma else 1)
            assert (kind, index) not in self.count, (kind, index)
            self.count[(kind, index)] = self.per[kind]
        self.ops.append((self.stage, engine, kind, make, list(waits), 16 if dma else 1, apart))

    def emit(self, name, engine, sems, row_of, last=False):
        for stage, eng, kind, make, waits, amount, apart in self.ops:
            if eng != name or stage not in row_of:
                continue
            row = row_of[stage]
            least = {}
            for w in waits:
                key, back = w if isinstance(w[1], Back) else (w, Back(0))
                if back.runs < 0 and last:
                    continue
                for k in self.final[key[1]] if key[0] == "bank" else [key]:
                    at = (1 - back.runs) * self.per[k[0]] + self.count[k]
                    least[k[0]] = max(at, least.get(k[0], at))
            for k, at in least.items():
                engine.wait_ge(sems[k], row * self.per[k] + at)
            if apart:
                engine.sem_inc(self.idle, 1)
            made = make(engine, row)
            if kind is not None:
                made.then_inc(sems[kind], amount)


class Back:
    def __init__(self, runs):
        self.runs = runs


def before(kind, index):
    return ((kind, index), Back(1))


def beside(kind, index):
    return ((kind, index), Back(-1))


def build(nc, x, qkv_w, qkv_b, proj_w, proj_b, g1, b1, g2, b2, fc1_w, fc1_b, fc2_w, fc2_b,
          alpha, w_gate, b_gate, W1m, b1m, W2m, b2m, W1e, b1e, W2e, b2e, out):
    f32, f32r, u32 = mybir.dt.float32, mybir.dt.float32r, mybir.dt.uint32
    ALU, ACT, AX = mybir.AluOpType, mybir.ActivationFunctionType, mybir.AxisListType

    ROWS, T, D = x.shape
    HID = fc1_w.shape[1]
    E = w_gate.shape[1]
    KD, KH, NT = D // P, HID // P, T // P
    HD, RAD = 16, 7
    HS = 4
    QB = P // HS
    NB = T // QB
    KW = 48
    G = 2
    UB = NB // 2
    NP_ = UB // 2
    LEFT = 8
    ZW = LEFT + T + 26
    NCH = 3 * KH
    NX = 2 * KH
    RING = 4

    with ExitStack() as ctx:
        def sb(name, shape, dt=f32):
            return ctx.enter_context(nc.sbuf_tensor(name, shape, dt))

        def pair(name, shape):
            return [sb(f"{name}_hi", shape, f32r), sb(f"{name}_lo", shape, f32r)]
        wqkv = pair("wqkv", [P, KD, 3 * D])
        wproj = pair("wproj", [P, KD, D])
        wf1 = pair("wf1", [P, KD, HID])
        wf2 = pair("wf2", [P, KH, D])
        wm1 = pair("wm1", [P, KD, HID])
        wm2 = pair("wm2", [P, KH, D])
        CW = KD * P + D
        raw = sb("raw", [P, RING, CW])
        wx = pair("wx", [P, RING, CW])
        xin = sb("xin", [P, NT, D])
        y = sb("y", [P, NT, D])
        sx = sb("sx", [P, NT, D])
        acc = sb("acc", [P, NT, D])
        tm = sb("tm", [P, NT, D])
        zT = pair("zT", [P, KD, ZW])
        z3 = pair("z3", [P, KD, T])
        kT = sb("kT", [P, ZW])
        qm = sb("qm", [P, 2, UB, HS * QB])
        kb = sb("kb", [P, 2, UB, G * KW])
        vb = sb("vb", [P, NB // 2, KD * G, P])
        pr = sb("pr", [P, 2, 2, G, 4, 64])
        pT = sb("pT", [P, G, NP_, P])
        zf = [pT[:, g, :, :].rearrange("p j q -> p (j q)") for g in range(G)]
        smax = sb("smax", [P, 2, UB * G])
        rinv = sb("rinv", [P, 4, 2, G, 4])
        hf = sb("hf", [P, 3, T])
        hr = pair("hr", [P, 2, T])
        ident = sb("ident", [P, P])
        band = sb("band", [P, KW])
        hmask = sb("hmask", [P, HS])
        gmask = sb("gmask", [P, G])
        one = sb("one", [1, 1])
        nil = sb("nil", [1, 1])
        ones = one[:, :].to_broadcast([1, P])
        keep = sb("keep", [P, 3])
        bv = sb("bv", [P, D])
        bproj = sb("bproj", [P, D])
        bfc2 = sb("bfc2", [P, D])
        b2all = sb("b2all", [E + 1, D])
        NSM = E * KH + 2 * KH + 2 * KD + 4 * KD
        small = pT[0:NSM, 0, 0, :]
        smallT = sb("smallT", [P, NSM])
        wg = sb("wg", [P, KD, E])
        bg = sb("bg", [1, E])
        iota = sb("iota", [1, E])
        mhalf = sb("mhalf", [P, 2 * NT])
        st = sb("st", [P, NT, 6])
        mv = sb("mv", [P, 3, NT, 2])
        ve = sb("ve", [P, 2 * NT])
        rs = sb("rs", [P, 4 * NT])
        msum = sb("msum", [P, KD])
        lg = sb("lg", [1, E])
        m8 = sb("m8", [1, 8])
        idx = sb("idx", [1, 8], u32)
        idf = sb("idf", [1, 2])
        tw = sb("tw", [1, 4])
        al = sb("al", [1, 2])
        NR = 3 * E + 3
        rrow = sb("rrow", [1, NR])
        bc = sb("bc", [P, NR])
        cb = sb("cb", [E + 1, 1])
        b1x = sb("b1x", [P, 2, KH])
        b1t = sb("b1t", [P, KH, E])

        psB = ctx.enter_context(nc.psum_tensor("psB", [P, 4, 512], f32))
        psA = ctx.enter_context(nc.psum_tensor("psA", [P, 4, 512], f32))

        oE, oM = 0, E * KH
        oF = oM + KH
        oQK = oF + KH
        oG1 = oQK + 2 * KD
        oB1, oG2, oB2 = oG1 + KD, oG1 + 2 * KD, oG1 + 3 * KD

        p = Plan()
        op = p.op

        def three(eng, dst, a, b, start, stop):
            for n, (u, v) in enumerate(((0, 0), (0, 1), (1, 0))):
                last = eng.matmul(dst, a[u], b[v], start=start and n == 0, stop=stop and n == 2)
            return last

        freed = {b: None for b in range(4)}

        def use(bank, readers):
            freed[bank] = readers

        def bankwait(bank):
            return [(("bank", bank), Back(1))] if freed[bank] is None else list(freed[bank])

        def ffn_weights(n):
            s, e, m = n % RING, n // KH, n % KH

            def load1(sp, row, s=s, e=e, m=m):
                ex = regs[e]
                return sp.dma_start(raw[:, s, 0:KD * P].rearrange("p (k n) -> p k n", k=KD),
                                    W1e[bass.ds(ex, 1), :, m * P:(m + 1) * P].rearrange("a (k p) n -> p (a k) n", p=P))

            def load2(sp, row, s=s, e=e, m=m):
                ex = regs[e]
                return sp.dma_start(raw[:, s, KD * P:], W2e[bass.ds(ex, 1), m * P:(m + 1) * P, :].rearrange("a p n -> p (a n)"))
            free = [("w_hi", n - RING), ("w_lo", n - RING)] if n >= RING else [before("w_hi", NX - RING + n), before("w_lo", NX - RING + n)]
            op("sp", f"raw{s}", (n, 0), load1, free, dma=True)
            op("sp", f"raw{s}", (n, 1), load2, dma=True)

        def ffn_split(n):
            s = n % RING
            free = ("down", KH + n - RING) if n >= RING else before("down", NCH - RING + n)
            op("pool", "w_hi", n, lambda g, r, s=s: g.tensor_scalar(wx[0][:, s, :], raw[:, s, :], 1.0, 0.0, ALU.mult, ALU.add),
               [(f"raw{s}", (n, 1)), free], apart=True)
            op("pool", "w_lo", n, lambda g, r, s=s: g.tensor_tensor(wx[1][:, s, :], raw[:, s, :], wx[0][:, s, :].bitcast(f32), ALU.subtract),
               [("w_hi", n)])

        def chunk_weights(m):
            if m < KH:
                return ([[w[:, k, m * P:(m + 1) * P] for w in wm1] for k in range(KD)], [w[:, m, :] for w in wm2])
            s = (m - KH) % RING
            return ([[w[:, s, k * P:(k + 1) * P] for w in wx] for k in range(KD)], [w[:, s, KD * P:] for w in wx])

        def h_split(kinds, m, pos, fpos, up_key, src, func, bias, h_free, t_free):
            op("act", kinds[0], m, lambda a, r: a.activation(hf[:, fpos, :], src, func, bias=bias), [up_key] + t_free)
            op("act", kinds[1], m, lambda a, r: a.activation(hr[0][:, pos, :], hf[:, fpos, :], ACT.Copy),
               [(kinds[0], m)] + h_free)
            op("dve", kinds[2], m, lambda v, r: v.tensor_tensor(hr[1][:, pos, :], hf[:, fpos, :], hr[0][:, pos, :].bitcast(f32), ALU.subtract),
               [(kinds[1], m)])

        def ffn_up(m):
            w1, _ = chunk_weights(m)
            waits = [("z3_lo", 1)] if m == 0 else []
            if m >= KH:
                waits += [("w_lo", m - KH)]
            waits += [("gelu", m - 2)] if m >= 2 else [before("gelu", NCH - 2 + m)]

            def mm(pe, r, m=m):
                for k in range(KD):
                    last = three(pe, psB[:, m % 2, :], w1[k], [z[:, k, :] for z in z3], k == 0, k == KD - 1)
                return last
            op("pe", "up", m, mm, waits)

        SPLIT = 20
        TR3 = 32
        order = [("f", m) for m in range(SPLIT)] + [("m", m) for m in range(KH)] + [("f", m) for m in range(SPLIT, NCH)]

        def ring_free(q, depth, ffn_kind, mlp_kind):
            me, m = order[q]
            prev, n = order[q - depth]
            if me == "m":
                return [(mlp_kind, n)] if prev == "m" else [before(ffn_kind, n)]
            own = [(ffn_kind, m - depth)] if m >= depth else []
            if q < depth:
                return [before(ffn_kind, NCH - depth + q)]
            return [beside(mlp_kind, n)] + own if prev == "m" else [(ffn_kind, n)]

        def hidden_free(q):
            return ring_free(q, 2, "down", "mdown"), ring_free(q, 3, "h_lo", "mh_lo")

        def ffn_hidden(m, q):
            if m < KH:
                bias = smallT[:, oM + m:oM + m + 1]
            else:
                bias = b1x[:, (m - KH) // KH, m % KH:m % KH + 1]
            h_free, t_free = hidden_free(q)
            h_split(("gelu", "h_hi", "h_lo"), m, q % 2, q % 3, ("up", m), psB[:, m % 2, :], ACT.Gelu_apprx_tanh, bias,
                    h_free, t_free + ([("b1x", 1)] if m == KH else []))

        def ffn_down(m, q):
            _, w2 = chunk_weights(m)
            f, j = divmod(m, KH)
            waits = [("h_lo", m)]
            if j == 0:
                waits += [("acc", (f - 1, 1))] if f else [before("acc", (2, 1))]

            def mm(pe, r, j=j, m=m):
                for i in range(NT):
                    a = [h[:, q % 2, i * P:(i + 1) * P] for h in hr]
                    last = three(pe, psB[:, 2 + i // 2, (i % 2) * D:(i % 2 + 1) * D], a, w2,
                                 j == 0 and i % 2 == 0, j == KH - 1 and i % 2 == 1)
                return last
            op("pe", "down", m, mm, waits)
            if j == KH - 1:
                for h in range(2):
                    waits = [("down", m)] + ([("acc", (f - 1, h))] if f else [("acc0", 0)])
                    c = bc[:, 3 * E + f:3 * E + f + 1]
                    sl = acc[:, 2 * h:2 * h + 2, :].rearrange("p i n -> p (i n)")
                    op("dve", "acc", (f, h), lambda v, r, h=h, c=c, sl=sl: v.scalar_tensor_tensor(
                        sl, psB[:, 2 + h, :], c, sl, ALU.mult, ALU.add), waits)

        regs = {}

        def route_load():
            def load(sp, row):
                for e in range(2):
                    regs[e] = sp.value_load(idx[0:1, e:e + 1], min_val=0, max_val=E - 1)
            op("sp", None, None, lambda sp, row: load(sp, row), [("idx", 0)], apart=True)

        def route_bcast():
            b = 1
            def mm(pe, r):
                pe.matmul(psA[:, b, 0:NR], ones, rrow[:, :], start=True, stop=True)
                return pe.matmul(psA[0:E + 1, b, 256:257], rrow[:, 2 * E:3 * E + 1], one[:, :], start=True, stop=True)
            op("pe", "route1", 0, mm, [("rrow", 6), ("bank", b)])
            op("dve", "cb", 0, lambda v, r: v.tensor_copy(cb[:, :], psA[0:E + 1, b, 256:257]),
               [("route1", 0), before("route2", 0)])
            op("dve", "bc", 0, lambda v, r: v.tensor_copy(bc[:, :], psA[:, b, 0:NR]), [before("acc", (2, 1)), before("b1x", 1)])

        def route_b1():
            for k in range(2):
                op("dve", "b1t", k, lambda v, r, k=k: v.tensor_tensor(
                    b1t[:, :, :], smallT[:, oE:oE + E * KH].rearrange("p (e c) -> p c e", e=E),
                    bc[:, k * E:(k + 1) * E].unsqueeze(1).to_broadcast([P, KH, E]), ALU.mult),
                   [("bc", 0)] + ([("b1x", 0)] if k else []))
                op("dve", "b1x", k, lambda v, r, k=k: v.tensor_reduce(b1x[:, k, :], b1t[:, :, :], AX.X, ALU.add),
                   [("b1t", k), before("gelu", NCH - 1)])

        def route_bias():
            b = 1
            op("pe", "route2", 0, lambda pe, r: pe.matmul(psA[:, b, 0:D], cb[:, :].to_broadcast([E + 1, P]), b2all[:, :], start=True, stop=True),
               [("cb", 0), ("bc", 0)])
            op("dve", "acc0", 0, lambda v, r: v.tensor_tensor(
                acc[:, :, :], sx[:, :, :], psA[:, b, 0:D].unsqueeze(1).to_broadcast([P, NT, D]), ALU.add),
               [("route2", 0), before("store", 0), ("x2", 1)])
            use(b, [before("acc0", 0)])

        def norm_before(kind, i, n):
            return before(kind, (2, i) if i is not None else 2) if n == 1 else \
                (kind, (1 - n // 2, i) if i is not None else 1 - n // 2)

        def stats(n, src, ready):
            for i in range(NT):
                op("dve", "st", (n, i), lambda v, r, i=i: v.bn_stats(st[:, i, :], src[:, i, :]),
                   (ready[i] if i < len(ready) else []) + [norm_before("mv", i, n)])
            for i in range(NT):
                op("dve", "mv", (n, i), lambda v, r, i=i, n=n: v.bn_aggr(mv[:, n, i, :], st[:, i, :]),
                   [("st", (n, i))] + ([before("rstd", n)] if i == 0 else []), apart=True)

        def power(n, adds, free):
            w = len(adds) * NT
            at = (0, 2 * NT, 3 * NT)[n]
            for j, (a_, b_) in enumerate(adds):
                op("pool", "vare", (n, j), lambda g, r, j=j, a_=a_, b_=b_: g.tensor_scalar(
                    ve[:, j * NT:(j + 1) * NT], mv[:, n, :, 1], a_, b_, ALU.mult, ALU.add),
                   [("mv", (n, NT - 1)), norm_before("rstd", None, n)], apart=True)
            op("pool", "rstd", n, lambda g, r: g.tensor_tensor(rs[:, at:at + w], ve[:, 0:w], mhalf[:, 0:w], ALU.pow),
               [("vare", (n, len(adds) - 1))] + free)
            return rs[:, at:at + w]

        def norm1_stats():
            stats(0, xin, [[("xload", 0)]])

        def norm1_power():
            power(0, [(1.0, EPS), (1.0 + EPS, EPS * EPS)], [("y", NT - 1)])

        def norm1_z():
            for i in range(NT):
                op("dve", "z", (0, i), lambda v, r, i=i: v.tensor_scalar(
                    tm[:, i, :], xin[:, i, :], mv[:, 0, i, 0:1], rs[:, NT + i:NT + i + 1], ALU.subtract, ALU.mult),
                   [("rstd", 0), ("tr3", 1)] if i == 0 else [])

        def first_norm1():
            for i in range(NT):
                op("dve", "st0", i, lambda v, r, i=i: v.bn_stats(st[:, i, :], xin[:, i, :]))
                op("dve", "mv0", i, lambda v, r, i=i: v.bn_aggr(mv[:, 0, i, :], st[:, i, :]), [("st0", i)], apart=True)
            for j, (a_, b_) in enumerate(((1.0, EPS), (1.0 + EPS, EPS * EPS))):
                op("pool", "vare0", j, lambda g, r, j=j, a_=a_, b_=b_: g.tensor_scalar(
                    ve[:, j * NT:(j + 1) * NT], mv[:, 0, :, 1], a_, b_, ALU.mult, ALU.add), [("mv0", NT - 1)], apart=True)
            op("pool", "rstd0", 0, lambda g, r: g.tensor_tensor(rs[:, 0:2 * NT], ve[:, :], mhalf[:, :], ALU.pow), [("vare0", 1)])

        def first_norm1_z():
            for i in range(NT):
                op("dve", "z0", i, lambda v, r, i=i: v.tensor_scalar(
                    tm[:, i, :], xin[:, i, :], mv[:, 0, i, 0:1], rs[:, NT + i:NT + i + 1], ALU.subtract, ALU.mult),
                   [("rstd0", 0)] if i == 0 else [])
            op("pe", None, None, lambda pe, r: None, [("z0", NT - 1)])

        def norm1_y():
            for i in range(NT):
                op("dve", "y", i, lambda v, r, i=i: v.tensor_scalar(
                    y[:, i, :], xin[:, i, :], mv[:, 0, i, 0:1], rs[:, i:i + 1], ALU.subtract, ALU.mult),
                   [before("sx", 0), before("rstd", 0)] if i == 0 else [])
            op("pool", "yb", 0, lambda g, r: g.tensor_tensor(
                y[:, :, :], y[:, :, :], bproj[:, :].unsqueeze(1).to_broadcast([P, NT, D]), ALU.add), [("y", NT - 1)])

        def transposes(kind, c, bank, waits):
            def mm(pe, r):
                for i in range(NT):
                    last = pe.transpose(psA[:, bank, i * P:(i + 1) * P], tm[:, i, c * P:(c + 1) * P], ident[:, :])
                return last
            op("pe", kind, c, mm, waits + bankwait(bank))

        def split_T(kind, c, bank, src_key, gain, bias, dst, off, free, banks_reader):
            op("act", kind + "_f", c, lambda a, r: a.activation(zf[c], psA[:, bank, :], ACT.Identity, bias=bias, scale=gain),
               [src_key, banks_reader])
            use(bank, [(kind + "_f", c)])
            op("act", kind + "_hi", c, lambda a, r: a.activation(dst[0][:, c, off:off + T], zf[c], ACT.Copy),
               [(kind + "_f", c)] + free)
            op("dve", kind + "_lo", c, lambda v, r: v.tensor_tensor(
                dst[1][:, c, off:off + T], zf[c], dst[0][:, c, off:off + T].bitcast(f32), ALU.subtract),
               [(kind + "_hi", c)])

        def split_plain(kind, c, bank, src_key, dst, off, free, accum=None):
            op("act", kind + "_hi", c, lambda a, r: a.activation(dst[0][:, c, off:off + T], psA[:, bank, :], ACT.Identity, accum_out=accum)
               if accum is not None else a.activation(dst[0][:, c, off:off + T], psA[:, bank, :], ACT.Identity),
               [src_key] + free)
            op("dve", kind + "_lo", c, lambda v, r: v.tensor_tensor(
                dst[1][:, c, off:off + T], psA[:, bank, :], dst[0][:, c, off:off + T].bitcast(f32), ALU.subtract),
               [(kind + "_hi", c)])
            use(bank, [(kind + "_lo", c)])

        def tr1(c):
            transposes("tr1", c, 2 + c, [before("z", (0, NT - 1))])
            zf_free = before("t2_lo", c)
            split_T("t1", c, 2 + c, ("tr1", c), smallT[:, oG1 + c:oG1 + c + 1], smallT[:, oB1 + c:oB1 + c + 1],
                    zT, LEFT, [before("mup", KH - 1)], zf_free)

        q_bank, k_bank = (3, 3), (0, 3)

        def project_qk(c, which, bank):
            col = which * D + c * P

            def mm(pe, r):
                for k in range(KD):
                    last = three(pe, psA[:, bank, :], [w[:, k, col:col + P] for w in wqkv],
                                 [z[:, k, LEFT:LEFT + T] for z in zT], k == 0, k == KD - 1)
                return last
            op("pe", "qk", (c, which), mm, [("t1_lo", 1)] + bankwait(bank))

        def keys(c):
            project_qk(c, 1, k_bank[c])
            j = KD + c
            op("act", "kT", c, lambda a, r: a.activation(
                kT[:, LEFT:LEFT + T], psA[:, k_bank[c], :], ACT.Identity, bias=smallT[:, oQK + j:oQK + j + 1]),
               [("qk", (c, 1)), ("kb", (1, 1)) if c else before("kb", (3, 1))])
            use(k_bank[c], [("kT", c)])
            for th in range(2):
                u = 2 * c + th
                first = kT[:, LEFT - RAD + th * UB * QB:LEFT - RAD + th * UB * QB + 1]
                win = bass.AP(first.tensor, first.offset, [first.ap[0], [QB, UB], [1, KW]])
                for g in range(G):
                    op("pool", "kb", (u, g), lambda e, r, th=th, g=g, win=win: e.tensor_scalar(
                        kb[:, th, :, g * KW:(g + 1) * KW], win, gmask[:, g:g + 1], None, ALU.mult),
                       [("kT", c), ("score", (u - 2, 1)) if c else before("score", (u + 2, 1))], apart=True)

        def queries(c):
            project_qk(c, 0, q_bank[c])

        def query_blocks(u):
            c, th = divmod(u, 2)
            for s in range(HS):
                op("dve", "qm", (u, s), lambda v, r, s=s: v.tensor_scalar(
                    qm[:, th, :, s * QB:(s + 1) * QB],
                    psA[:, q_bank[c], th * UB * QB:(th + 1) * UB * QB].rearrange("p (b q) -> p b q", q=QB),
                    smallT[:, oQK + c:oQK + c + 1], hmask[:, s:s + 1], ALU.add, ALU.mult),
                   [("qk", (c, 0)), ("score", (u - 2, 1)) if c else before("score", (u + 2, 1))])
            use(q_bank[c], [("qm", (u, HS - 1))])

        def zeros():
            op("pool", "zeros", 0, lambda g, r: g.memset(pr[:, :, :, :, :, :], 0.0))
            op("pool", "zeros", 1, lambda g, r: g.memset(vb[:, :, :, :], 0.0))
            op("dve", None, None, lambda v, r: None, [("zeros", 1)])

        def values(n):
            bank = 2

            def mm(pe, r):
                for j in range(2):
                    base = LEFT - RAD + (4 * n + j) * QB
                    for k in range(KD):
                        last = three(pe, psA[:, bank, j * D:(j + 1) * D], [z[:, k, base:base + P] for z in zT],
                                     [w[:, k, 2 * D:] for w in wqkv], k == 0, k == KD - 1)
                return last
            op("pe", "val", n, mm, [("t1_lo", 1)] + bankwait(bank))
            for j in range(2):
                i = 2 * n + j
                kc = 0 if i == 0 else 2 if i == NB // 2 - 1 else 1
                for s in range(2):
                    rows = slice(64 * s, 64 * s + 64)
                    op("dve", "vb", (i, s), lambda v, r, i=i, j=j, s=s, rows=rows, kc=kc: v.scalar_tensor_tensor(
                        vb[rows, i, :, 64 * s:64 * s + 64], bv[rows, :].rearrange("p (g n) -> p g n", n=64),
                        keep[rows, kc:kc + 1], psA[rows, bank, j * D:(j + 1) * D].rearrange("p (g n) -> p g n", n=64),
                        ALU.mult, ALU.add),
                       [("val", n), before("av", (3, 1))])
            use(bank, [("vb", (2 * n + 1, 1))])

        def place(j):
            return 2 * (j % 2) + j // 2

        def score(u, b0):
            th = u % 2
            for h in range(2):
                bank = b0 + h

                def mm(pe, r, h=h, bank=bank):
                    for j in range(4):
                        b = 4 * h + j
                        dst = psA[:, bank, 0:4 * G * KW].rearrange("p (g b k) -> p g b k", g=G, k=KW)[:, :, place(j), :]
                        last = pe.matmul(dst, qm[:, th, b, :], kb[:, th, b, :].rearrange("p (g k) -> p g k", g=G),
                                         start=True, stop=True)
                    return last
                op("pe", "score", (u, h), mm, [("qm", (u, HS - 1)), ("kb", (u, 1))] + bankwait(bank))
                op("dve", "masked", (u, h), lambda v, r, h=h, bank=bank: v.scalar_tensor_tensor(
                    pr[:, th, h, :, :, 0:KW].rearrange("p g b k -> p (g b) k"),
                    psA[:, bank, 0:4 * G * KW].rearrange("p (n k) -> p n k", k=KW), HD ** -0.5,
                    band[:, :].unsqueeze(1).to_broadcast([P, 4 * G, KW]), ALU.mult, ALU.add),
                   [("score", (u, h)), ("trp", (u - 2, 1)) if u >= 2 else before("trp", (u + 2, 1))])
                use(bank, [("masked", (u, h))])

        def unit_scores(u):
            return pr[:, u % 2, :, :, :, 0:KW].rearrange("p t g b k -> p (t g b) k")

        def shift(u):
            th, s = u % 2, unit_scores(u)
            op("dve", "smax", u, lambda v, r: v.tensor_reduce(smax[:, th, :], s, AX.X, ALU.max), [("masked", (u, 1))])
            op("dve", "shift", u, lambda v, r: v.tensor_tensor(
                s, s, smax[:, th, :].unsqueeze(2).to_broadcast([P, UB * G, KW]), ALU.subtract), [("smax", u)])

        def exp(u):
            s = unit_scores(u)
            op("act", "exp", u, lambda a, r: a.activation(s, s, ACT.Exp), [("shift", u)])

        def sums(u):
            th, s = u % 2, unit_scores(u)
            op("dve", "ssum", u, lambda v, r: v.tensor_reduce(smax[:, th, :], s, AX.X, ALU.add), [("exp", u)])
            op("dve", "rinv", u, lambda v, r: v.reciprocal(
                rinv[:, u, :, :, :].rearrange("p t g b -> p (t g b)"), smax[:, th, :]), [("ssum", u)])

        def probT(u, b0):
            th = u % 2
            for g in range(G):
                bank = b0 + g

                def mm(pe, r, g=g, bank=bank):
                    for j in range(NP_):
                        last = pe.transpose(psA[:, bank, j * P:(j + 1) * P], pr[:, th, j // 2, g, 2 * (j % 2):2 * (j % 2) + 2, :].rearrange("p b k -> p (b k)"), ident[:, :])
                    return last
                op("pe", "trp", (u, g), mm, [("exp", u)] + bankwait(bank))
                op("act", "pT", (u, g), lambda a, r, g=g, bank=bank: a.activation(
                    pT[:, g, :, :].rearrange("p j q -> p (j q)"), psA[:, bank, :], ACT.Copy),
                   [("trp", (u, g)), ("av", (u - 1, g)) if u else before("av", (3, g))])
                use(bank, [("pT", (u, g))])

        def attend(u, b0):
            c, th = divmod(u, 2)
            for g in range(G):
                bank = b0 + g

                def mm(pe, r, g=g, bank=bank):
                    for j in range(NP_):
                        last = pe.matmul(psA[:, bank, j * P:(j + 1) * P], pT[:, g, j, :],
                                         vb[:, th * NP_ + j, c * G + g, :], start=True, stop=True)
                    return last
                op("pe", "av", (u, g), mm, [("pT", (u, g)), ("vb", (th * NP_ + NP_ - 1, 1))] + bankwait(bank))
            for h in range(HS):
                for b in range(P // QB):
                    src = psA[QB * h:QB * h + QB, b0:b0 + 2, :].rearrange(
                        "p g (t j s n) -> p g t j s n", t=2, j=2, s=2)[:, :, :, b % 2, b // 2, HD * h:HD * h + HD]
                    f0 = c * P + HD * h
                    dst = tm[QB * b:QB * b + QB, 2 * th:2 * th + 2, c * P:(c + 1) * P].rearrange(
                        "p t (g n) -> p g t n", g=G)[:, :, :, HD * h:HD * h + HD]
                    w = rinv[QB * h:QB * h + QB, u, :, :, :].rearrange("p t g b -> p g t b")[:, :, :, place(b)]\
                        .unsqueeze(3).to_broadcast([QB, G, 2, HD])
                    op("dve", "att", (u, h, b), lambda v, r, src=src, dst=dst, w=w: v.tensor_tensor(dst, src, w, ALU.mult),
                       [("av", (u, 1)), ("rinv", u), ("tr1", 1)] if (h, b) == (0, 0) else [])
            for g in range(G):
                use(b0 + g, [("att", (u, HS - 1, P // QB - 1))])

        def attT(c, bank):
            transposes("trA", c, bank, [("att", (3, HS - 1, P // QB - 1))])
            split_plain("tA", c, bank, ("trA", c), zT, LEFT, [("val", NB // 4 - 1), ("qk", (1, 0))])

        def project(b0):
            for h in range(2):
                bank = b0 + h

                def mm(pe, r, h=h, bank=bank):
                    for j in range(2):
                        i = 2 * h + j
                        for k in range(KD):
                            last = three(pe, psA[:, bank, j * D:(j + 1) * D],
                                         [z[:, k, LEFT + i * P:LEFT + (i + 1) * P] for z in zT],
                                         [w[:, k, :] for w in wproj], k == 0, k == KD - 1)
                    return last
                op("pe", "proj", h, mm, [("tA_lo", 1)] + bankwait(bank))
                sl = y[:, 2 * h:2 * h + 2, :].rearrange("p i n -> p (i n)")
                op("dve", "x1", h, lambda v, r, bank=bank, sl=sl: v.tensor_tensor(sl, sl, psA[:, bank, :], ALU.add),
                   [("proj", h), ("yb", 0)])
                use(bank, [("x1", h)])

        def norm2_stats():
            stats(1, y, [[("x1", 0)], [], [("x1", 1)], []])
            power(1, [(1.0, EPS)], [before("z", (1, NT - 1))])

        def shortcut():
            op("pool", "sx", 0, lambda g, r: g.tensor_tensor(sx[:, :, :], xin[:, :, :], y[:, :, :], ALU.add),
               [("x1", 1), before("acc0", 0)])
            op("pool", "sxb", 0, lambda g, r: g.tensor_tensor(
                sx[:, :, :], sx[:, :, :], bfc2[:, :].unsqueeze(1).to_broadcast([P, NT, D]), ALU.add), [("sx", 0)])

        def norm2_apply():
            for i in range(NT):
                op("dve", "z", (1, i), lambda v, r, i=i: v.tensor_scalar(
                    tm[:, i, :], y[:, i, :], mv[:, 1, i, 0:1], rs[:, 2 * NT + i:2 * NT + i + 1], ALU.subtract, ALU.mult),
                   [("rstd", 1), ("trA", 1)] if i == 0 else [])

        def tr2(c, bank):
            transposes("tr2", c, bank, [("z", (1, NT - 1))])
            split_T("t2", c, bank, ("tr2", c), smallT[:, oG2 + c:oG2 + c + 1], smallT[:, oB2 + c:oB2 + c + 1],
                    zT, LEFT, [("proj", 1)], ("t1_lo", c))

        def mlp_up(m):
            def mm(pe, r):
                for k in range(KD):
                    last = three(pe, psA[:, m % 2, :], [w[:, k, m * P:(m + 1) * P] for w in wf1],
                                 [z[:, k, LEFT:LEFT + T] for z in zT], k == 0, k == KD - 1)
                return last
            op("pe", "mup", m, mm, [("t2_lo", 1)] + bankwait(m % 2))
            use(m % 2, [("mgelu", m)])

        def mlp_hidden(m, q):
            h_free, t_free = hidden_free(q)
            h_split(("mgelu", "mh_hi", "mh_lo"), m, q % 2, q % 3, ("mup", m), psA[:, m % 2, :], ACT.Gelu,
                    smallT[:, oF + m:oF + m + 1], h_free, t_free)

        def mlp_down(m, q):
            def mm(pe, r):
                for i in range(NT):
                    a = [h[:, q % 2, i * P:(i + 1) * P] for h in hr]
                    last = three(pe, psA[:, 2 + i // 2, (i % 2) * D:(i % 2 + 1) * D], a, [w[:, m, :] for w in wf2],
                                 m == 0 and i % 2 == 0, m == KH - 1 and i % 2 == 1)
                return last
            op("pe", "mdown", m, mm, [("mh_lo", m)] + (bankwait(2) + bankwait(3) if m == 0 else []))
            if m == KH - 1:
                for h in range(2):
                    sl = sx[:, 2 * h:2 * h + 2, :].rearrange("p i n -> p (i n)")
                    op("dve", "x2", h, lambda v, r, h=h, sl=sl: v.tensor_tensor(sl, sl, psA[:, 2 + h, :], ALU.add),
                       [("mdown", KH - 1), ("sxb", 0)])
                    use(2 + h, [("x2", h)])

        def xload():
            op("sp", "xload", 0, lambda sp, r: sp.dma_start(
                xin[:, :, :], x[bass.ds((r + 1) % ROWS, 1), :, :].rearrange("a (i p) n -> p (a i) n", p=P)),
               [("sx", 0), ("y", NT - 1)], dma=True)

        def norm3_stats():
            stats(2, sx, [[("x2", 0)], [], [("x2", 1)], []])
            power(2, [(1.0, EPS)], [before("z", (2, NT - 1))])

        def norm3_apply():
            for i in range(NT):
                op("dve", "z", (2, i), lambda v, r, i=i: v.tensor_scalar(
                    tm[:, i, :], sx[:, i, :], mv[:, 2, i, 0:1], rs[:, 3 * NT + i:3 * NT + i + 1], ALU.subtract, ALU.mult),
                   [("rstd", 2), ("tr2", 1)] if i == 0 else [])

        def tr3(c, bank):
            transposes("tr3", c, bank, [("z", (2, NT - 1))])
            split_plain("z3", c, bank, ("tr3", c), z3, 0, [before("up", NCH - 1), before("router", 0)], msum[:, c:c + 1])

        def router(bank):
            def mm(pe, r):
                for k in range(KD):
                    last = pe.matmul(psA[0:1, bank, 0:E], msum[:, k:k + 1], wg[:, k, :], start=k == 0, stop=k == KD - 1)
                return last
            op("pe", "router", 0, mm, [("z3_hi", 1)] + bankwait(bank))
            use(bank, [("lg", 0)])
            op("dve", "lg", 0, lambda v, r: v.scalar_tensor_tensor(
                lg[:, :], psA[0:1, bank, 0:E], 1.0 / T, bg[:, :], ALU.mult, ALU.add), [("router", 0)])
            op("dve", "m8", 0, lambda v, r: v.max(m8[:, :], lg[:, :]), [("lg", 0)], apart=True)
            op("dve", "idx", 0, lambda v, r: v.max_index(idx[:, :], m8[:, :], lg[:, :]), [("m8", 0), before(f"raw{RING - 1}", (NX - 1, 1))], apart=True)

        def route_row():
            op("dve", "tw", 0, lambda v, r: v.tensor_tensor(tw[:, 0:1], m8[:, 0:1], m8[:, 1:2], ALU.subtract), [("m8", 0)])
            op("act", "tanh", 0, lambda a, r: a.activation(tw[:, 1:2], tw[:, 0:1], ACT.Tanh, scale=0.5), [("tw", 0)])
            op("dve", "idf", 0, lambda v, r: v.tensor_copy(idf[:, :], idx[:, 0:2]), [("idx", 0)])
            for k in range(2):
                op("dve", "rrow", k, lambda v, r, k=k: v.tensor_scalar(
                    rrow[:, k * E:(k + 1) * E], iota[:, :], idf[:, k:k + 1], None, ALU.is_equal),
                   [("idf", 0), before("route1", 0)])
            for k in range(2):
                op("dve", "rrow", 2 + k, lambda v, r, k=k: v.tensor_scalar(
                    tw[:, 2 + k:3 + k], tw[:, 1:2], 0.5 - k, 0.5, ALU.mult, ALU.add), [("tanh", 0)])
            op("dve", "rrow", 4, lambda v, r: v.tensor_scalar(
                rrow[:, 3 * E + 1:3 * E + 3], tw[:, 2:4], al[:, 1:2], None, ALU.mult), [("rrow", 3)])
            op("dve", "rrow", 5, lambda v, r: v.tensor_scalar(
                rrow[:, 2 * E:3 * E], rrow[:, 0:E], rrow[:, 3 * E + 1:3 * E + 2], None, ALU.mult), [("rrow", 4)])
            op("dve", "rrow", 6, lambda v, r: v.scalar_tensor_tensor(
                rrow[:, 2 * E:3 * E], rrow[:, E:2 * E], rrow[:, 3 * E + 2:3 * E + 3], rrow[:, 2 * E:3 * E], ALU.mult, ALU.add),
               [("rrow", 5)])

        pieces = []
        qkv_v = qkv_w.rearrange("(k p) n -> p k n", p=P)
        for k in range(KD):
            for h in range(2):
                c = slice(h * 3 * D // 2, (h + 1) * 3 * D // 2)
                pieces.append((qkv_v[:, k, c], [w[:, k, c] for w in wqkv], None))
        pieces.append((proj_w.rearrange("(k p) n -> p k n", p=P), [w[:, :, :] for w in wproj], KD))

        def first_layer(w, dst):
            v = w.rearrange("(k p) n -> p k n", p=P)
            for k in range(KD):
                for h in range(HID // CW):
                    c = slice(h * CW, (h + 1) * CW)
                    pieces.append((v[:, k, c], [d[:, k, c] for d in dst], None))

        def second_layer(w, dst):
            v = w.rearrange("(m p) n -> p m n", p=P)
            n = CW // D
            for m in range(0, KH, n):
                pieces.append((v[:, m:m + n, :], [d[:, m:m + n, :] for d in dst], n))
        first_layer(fc1_w, wf1)
        second_layer(fc2_w, wf2)
        first_layer(W1m, wm1)
        second_layer(W2m, wm2)

        def raw_piece(n):
            _, dst, inner = pieces[n]
            width = 1
            for d in dst[0].shape[1:]:
                width *= d
            v = raw[:, n % RING, 0:width]
            return v.rearrange("p (k n) -> p k n", k=inner) if inner else v

        start_steps = []
        FIRST = 2 * KD

        def zero_pads():
            zeros()
        start_steps.append(zero_pads)

        def split_of(n):
            return ("p_lo" if n < FIRST else "g_lo", n)

        def weights(a, b):
            def f():
                for n in range(a, b):
                    s = n % RING
                    _, dst, _ = pieces[n]
                    op("sp", f"praw{s}", n, lambda sp, r, n=n: sp.dma_start(raw_piece(n), pieces[n][0]),
                       [split_of(n - RING)] if n >= RING else [], dma=True)
                    if n < FIRST:
                        op("act", "p_hi", n, lambda a, r, n=n, dst=dst: a.activation(dst[0], raw_piece(n), ACT.Copy), [(f"praw{s}", n)])
                        op("dve", "p_lo", n, lambda v, r, n=n, dst=dst: v.tensor_tensor(
                            dst[1], raw_piece(n), dst[0].bitcast(f32), ALU.subtract), [("p_hi", n)])
                    else:
                        op("pool", "g_hi", n, lambda g, r, n=n, dst=dst: g.tensor_scalar(
                            dst[0], raw_piece(n), 1.0, 0.0, ALU.mult, ALU.add), [(f"praw{s}", n)], apart=True)
                        op("pool", "g_lo", n, lambda g, r, n=n, dst=dst: g.tensor_tensor(
                            dst[1], raw_piece(n), dst[0].bitcast(f32), ALU.subtract), [("g_hi", n)])
            start_steps.append(f)
            return f

        def ready(n):
            def f():
                op("pe", None, None, lambda pe, r: None, [split_of(n - 1)])
            start_steps.append(f)
            return f

        def table(n, func):
            return lambda: op("act", "table", n, lambda a, r: a.activation(nil[:, :], one[:, :], func),
                              [("table", n - 1) if n else before("table", 2)])

        def both(f, *args):
            return lambda: [f(*a) for a in args]

        GELU_TANH = ACT.Gelu_apprx_tanh
        steps = {
            -1: [table(0, GELU_TANH), route_load],
            0: [both(tr1, (0,), (1,))],
            1: [route_row, ready(4)],
            2: [both(keys, (0,)), both(queries, (0,)), route_bcast, both(query_blocks, (0,)), weights(4, 7)],
            3: [route_bias, both(query_blocks, (1,)), zero_pads, both(values, (0,))],
            4: [both(score, (0, 0)), both(shift, (0,)), both(values, (1,)), norm1_y],
            5: [both(keys, (1,)), both(score, (1, 0)), both(shift, (1,)), weights(7, 13)],
            6: [both(exp, (0,), (1,)), both(queries, (1,)), both(query_blocks, (2,)), both(sums, (0,)), route_b1],
            7: [both(probT, (0, 0)), both(values, (2,)), both(sums, (1,))],
            8: [both(query_blocks, (3,)), both(score, (2, 0))],
            9: [both(shift, (2,)), both(attend, (0, 2)), both(probT, (1, 0))],
            10: [both(score, (3, 0)), both(shift, (3,)), both(values, (3,))],
            11: [both(exp, (2,), (3,)), both(attend, (1, 2)), weights(13, 21)],
            12: [both(probT, (2, 0)), both(sums, (2,), (3,))],
            13: [both(attend, (2, 2)), both(probT, (3, 0))],
            14: [both(attend, (3, 2))],
            15: [both(attT, (0, 0), (1, 1)), ready(5)],
            16: [both(project, (2,)), norm2_stats],
            17: [norm2_apply, table(1, ACT.Gelu)],
            18: [both(tr2, (0, 0), (1, 1)), ready(13)],
            SPLIT: [shortcut],
            SPLIT + 3: [xload],
            SPLIT + 6: [norm1_stats, norm1_power],
            SPLIT + 7: [table(2, GELU_TANH)],
            SPLIT + 9: [norm3_stats],
            SPLIT + 10: [norm3_apply],
            TR3: [both(tr3, (0, 0), (1, 1)), norm1_z],
            TR3 + 1: [both(router, (0,))],
        }
        route_steps = (route_load, route_row, route_bcast, route_b1, route_bias)

        def run_steps(s):
            for f in steps.get(s, ()):
                p.stage = "route" if f in route_steps else "start" if f in start_steps else "attn"
                f()

        p.stage = "first"
        first_norm1()
        weights(0, FIRST)()
        p.stage = "second"
        first_norm1_z()
        run_steps(-1)
        loads = 0
        for q in range(len(order) + 2):
            if q < len(order):
                kind, m = order[q]
                if kind == "f":
                    p.stage = "ffn"
                    while loads < NX and loads < m + RING + 1:
                        ffn_weights(loads)
                        loads += 1
                    if 3 <= m < 3 + RING:
                        ffn_split(m - 3)
                    ffn_up(m)
                else:
                    p.stage = "attn"
                    mlp_up(m)
            if q >= 2:
                kind, m = order[q - 2]
                p.stage = "ffn" if kind == "f" else "attn"
                (ffn_down if kind == "f" else mlp_down)(m, q - 2)
                if kind == "f" and KH <= m < NCH - RING:
                    ffn_split(m - KH + RING)
            if q < len(order):
                kind, m = order[q]
                p.stage = "ffn" if kind == "f" else "attn"
                (ffn_hidden if kind == "f" else mlp_hidden)(m, q)
            run_steps(q)
        p.stage = "start"
        for e in ("pe", "sp"):
            op(e, None, None, lambda eng, r: None, [split_of(len(pieces) - 1)])
        p.stage = "ffn"
        op("sp", "store", 0, lambda sp, r: sp.dma_start(
            out[bass.ds(r, 1), :, :].rearrange("a (i p) n -> p (a i) n", p=P), acc[:, :, :]), [("acc", (2, 1))], dma=True)
        p.final = freed

        sems = {k: ctx.enter_context(nc.semaphore(f"s_{k}")) for k in p.per}
        start = {k: ctx.enter_context(nc.semaphore(f"c_{k}")) for k in
                 ("x", "small", "rows", "pool", "dve", "smallT", "smallP")}

        p.idle = ctx.enter_context(nc.semaphore("c_idle"))

        def prime(engine, name):
            for k in p.per:
                if any(o[1] == name and o[2] == k for o in p.ops):
                    engine.sem_inc(sems[k], p.per[k])

        def runs(engine, name):
            p.emit(name, engine, sems, {"start": 0, "attn": 0})
            with engine.Fori(0, ROWS - 1) as i:
                p.emit(name, engine, sems, {"route": i, "ffn": i, "attn": i + 1})
            p.emit(name, engine, sems, {"route": ROWS - 1, "ffn": ROWS - 1}, last=True)

        def first(engine, name, stage="first"):
            p.emit(name, engine, sems, {stage: 0})

        block = ctx.enter_context(nc.Block())

        @block.sync
        def _(sp):
            prime(sp, "sp")

            sp.dma_start(xin[:, :, :], x[0, :, :].rearrange("(i p) n -> p i n", p=P)).then_inc(start["x"], 16)
            first(sp, "sp")
            rows = [(b1e.rearrange("e (c p) -> (e c) p", p=P), oE, E * KH), (b1m.rearrange("(c p) -> c p", p=P), oM, KH),
                    (fc1_b.rearrange("(c p) -> c p", p=P), oF, KH), (qkv_b.rearrange("(c p) -> c p", p=P)[0:2 * KD, :], oQK, 2 * KD),
                    (g1.rearrange("(c p) -> c p", p=P), oG1, KD), (b1.rearrange("(c p) -> c p", p=P), oB1, KD),
                    (g2.rearrange("(c p) -> c p", p=P), oG2, KD), (b2.rearrange("(c p) -> c p", p=P), oB2, KD)]
            for src, at, n in rows:
                sp.dma_start(small[at:at + n, :], src).then_inc(start["small"], 16)
            row = lambda a: a.rearrange("(o n) -> o n", o=1)
            for src, dst in ((qkv_b[2 * D:3 * D], bv), (proj_b, bproj), (fc2_b, bfc2)):
                sp.dma_start(dst[:, :], row(src).to_broadcast([P, D])).then_inc(start["rows"], 16)
            sp.dma_start(b2all[0:E, :], b2e).then_inc(start["rows"], 16)
            sp.dma_start(b2all[E:E + 1, :], row(b2m)).then_inc(start["rows"], 16)
            sp.dma_start(wg[:, :, :], w_gate.rearrange("(k p) e -> p k e", p=P)).then_inc(start["rows"], 16)
            sp.dma_start(bg[:, :], row(b_gate)).then_inc(start["rows"], 16)
            sp.dma_start(al[:, 0:1], row(alpha)).then_inc(start["rows"], 16)
            sp.wait_ge(start["smallT"], 1)
            runs(sp, "sp")
            sp.wait_ge(sems["store"], (ROWS + 1) * p.per["store"])

        @block.gpsimd
        def _(g):
            prime(g, "pool")
            n = 0

            def link(ins):
                nonlocal n
                n += 1
                ins.then_inc(start["pool"], 1)
                g.wait_ge(start["pool"], n)
            link(g.memset(mhalf[:, :], -0.5))
            link(g.memset(one[:, :], 1.0))
            link(g.memset(ident[:, :], 0.0))
            link(g.affine_select(out=ident[:, :], in_=ident[:, :], compare_op=ALU.not_equal, fill=1.0, base=0,
                                 pattern=[[-1, P]], channel_multiplier=1))
            first(g, "pool")
            link(g.memset(band[:, :], 0.0))
            for h in range(HS):
                v = band[QB * h:QB * h + QB, :]
                link(g.affine_select(out=v, in_=v, compare_op=ALU.is_ge, fill=-1e30, base=0, pattern=[[1, KW]], channel_multiplier=-1))
                link(g.affine_select(out=v, in_=v, compare_op=ALU.is_ge, fill=-1e30, base=2 * RAD, pattern=[[-1, KW]], channel_multiplier=1))
            link(g.memset(hmask[:, :], 1.0))
            for h in range(2):
                v = hmask[64 * h:64 * h + 64, :]
                link(g.affine_select(out=v, in_=v, compare_op=ALU.is_ge, fill=0.0, base=0, pattern=[[-HD, HS]], channel_multiplier=1))
                link(g.affine_select(out=v, in_=v, compare_op=ALU.is_ge, fill=0.0, base=HD - 1, pattern=[[HD, HS]], channel_multiplier=-1))
            link(g.memset(gmask[:, :], 1.0))
            link(g.affine_select(out=gmask[:, 0:1], in_=gmask[:, 0:1], compare_op=ALU.is_ge, fill=0.0, base=63, pattern=[[0, 1]], channel_multiplier=-1))
            link(g.affine_select(out=gmask[:, 1:2], in_=gmask[:, 1:2], compare_op=ALU.is_ge, fill=0.0, base=-64, pattern=[[0, 1]], channel_multiplier=1))
            link(g.memset(keep[:, :], 1.0))
            link(g.affine_select(out=keep[:, 0:1], in_=keep[:, 0:1], compare_op=ALU.is_ge, fill=0.0, base=-RAD, pattern=[[0, 1]], channel_multiplier=1))
            link(g.affine_select(out=keep[:, 2:3], in_=keep[:, 2:3], compare_op=ALU.is_ge, fill=0.0, base=64 + QB + RAD - 1, pattern=[[0, 1]], channel_multiplier=-1))
            link(g.iota(iota[:, :], pattern=[[1, E]], base=0, channel_multiplier=0, allow_small_or_imprecise_dtypes=True))
            g.wait_ge(start["rows"], 16 * 8)
            g.wait_ge(start["dve"], len(zT) * 2 + 2)
            runs(g, "pool")
            assert n == N_POOL, n

        @block.vector
        def _(v):
            prime(v, "dve")
            zeros = [kT[:, 0:LEFT], kT[:, LEFT + T:ZW]]
            for z in zT:
                zeros += [z[:, :, 0:LEFT].bitcast(f32), z[:, :, LEFT + T:ZW].bitcast(f32)]
            for z in zeros:
                v.memset(z, 0.0).then_inc(start["dve"], 1)
            v.wait_ge(start["x"], 16)
            first(v, "dve")
            v.wait_ge(start["rows"], 16 * 8)
            v.tensor_scalar(rrow[:, 3 * E:3 * E + 1], al[:, 0:1], 0.1, 1.0, ALU.max, ALU.min).then_inc(start["dve"], 1)
            v.wait_ge(start["dve"], len(zeros) + 1)
            v.tensor_scalar(al[:, 1:2], rrow[:, 3 * E:3 * E + 1], -1.0, 1.0, ALU.mult, ALU.add).then_inc(start["dve"], 1)
            v.wait_ge(start["dve"], len(zeros) + 2)
            v.wait_ge(start["smallP"], 1)
            v.tensor_copy(smallT[:, :], psA[:, 0, 0:NSM]).then_inc(start["smallT"], 1)
            v.wait_ge(start["smallT"], 1)
            first(v, "dve", "second")
            v.wait_ge(start["pool"], N_POOL)
            runs(v, "dve")

        @block.scalar
        def _(a):
            prime(a, "act")
            first(a, "act")
            a.wait_ge(start["smallT"], 1)
            a.wait_ge(start["pool"], 4)
            a.wait_ge(start["dve"], len(zT) * 2 + 2)
            runs(a, "act")

        @block.tensor
        def _(pe):
            prime(pe, "pe")
            pe.wait_ge(start["small"], 16 * 8)
            pe.wait_ge(start["pool"], 4)
            pe.transpose(psA[:, 0, 0:NSM], small[:, :], ident[0:NSM, 0:NSM]).then_inc(start["smallP"], 1)
            pe.wait_ge(start["smallT"], 1)
            pe.wait_ge(start["rows"], 16 * 8)
            first(pe, "pe", "second")
            runs(pe, "pe")


_INS = ['L0_attn_x', 'L0_attn_qkv_w', 'L0_attn_qkv_b', 'L0_attn_proj_w', 'L0_attn_proj_b', 'L0_attn_norm1_g',
        'L0_attn_norm1_b', 'L0_attn_norm2_g', 'L0_attn_norm2_b', 'L0_attn_fc1_w', 'L0_attn_fc1_b', 'L0_attn_fc2_w',
        'L0_attn_fc2_b', 'L0_ffn_alpha', 'L0_ffn_w_gate', 'L0_ffn_b_gate', 'L0_ffn_W1m', 'L0_ffn_b1m', 'L0_ffn_W2m',
        'L0_ffn_b2m', 'L0_ffn_W1e', 'L0_ffn_b1e', 'L0_ffn_W2e', 'L0_ffn_b2e']


def kernel(**inputs):
    import numpy as np
    import concourse.bacc as bacc
    from concourse.bass_utils import run_bass_kernel_spmd

    nc = bacc.Bacc("TRN2", target_bir_lowering=False, num_devices=1)
    arrays, args = {}, []
    for name in _INS:
        a = np.ascontiguousarray(inputs[name])
        if a.ndim == 0:
            a = a.reshape(1)
        arrays["in_" + name] = a
        args.append(nc.dram_tensor("in_" + name, a.shape, mybir.dt.from_np(a.dtype), kind="ExternalInput").ap())
    shape = arrays["in_L0_attn_x"].shape
    args.append(nc.dram_tensor("out_x", shape, mybir.dt.float32, kind="ExternalOutput").ap())
    build(nc, *args)
    r = run_bass_kernel_spmd(nc, [arrays], core_ids=[0])
    return r.results[0]["out_x"]
```

```python
from contextlib import ExitStack

import concourse.bass as bass
from concourse import mybir

P = 128
EPS = 1e-5
N_POOL = 25


class Plan:

    def __init__(self):
        self.ops, self.count, self.per, self.stage, self.final = [], {}, {}, None, {}

    def op(self, engine, kind, index, make, waits=(), dma=False, apart=False):
        if kind is not None:
            self.per[kind] = self.per.get(kind, 0) + (16 if dma else 1)
            assert (kind, index) not in self.count, (kind, index)
            self.count[(kind, index)] = self.per[kind]
        self.ops.append((self.stage, engine, kind, make, list(waits), 16 if dma else 1, apart))

    def emit(self, name, engine, sems, row_of, last=False):
        for stage, eng, kind, make, waits, amount, apart in self.ops:
            if eng != name or stage not in row_of:
                continue
            row = row_of[stage]
            least = {}
            for w in waits:
                key, back = w if isinstance(w[1], Back) else (w, Back(0))
                if back.runs < 0 and last:
                    continue
                for k in self.final[key[1]] if key[0] == "bank" else [key]:
                    at = (1 - back.runs) * self.per[k[0]] + self.count[k]
                    least[k[0]] = max(at, least.get(k[0], at))
            for k, at in least.items():
                engine.wait_ge(sems[k], row * self.per[k] + at)
            if apart:
                engine.sem_inc(self.idle, 1)
            made = make(engine, row)
            if kind is not None:
                made.then_inc(sems[kind], amount)


class Back:
    def __init__(self, runs):
        self.runs = runs


def before(kind, index):
    return ((kind, index), Back(1))


def beside(kind, index):
    return ((kind, index), Back(-1))


def build(nc, x, qkv_w, qkv_b, proj_w, proj_b, g1, b1, g2, b2, fc1_w, fc1_b, fc2_w, fc2_b,
          alpha, w_gate, b_gate, W1m, b1m, W2m, b2m, W1e, b1e, W2e, b2e, out):
    f32, f32r, u32 = mybir.dt.float32, mybir.dt.float32r, mybir.dt.uint32
    ALU, ACT, AX = mybir.AluOpType, mybir.ActivationFunctionType, mybir.AxisListType

    ROWS, T, D = x.shape
    HID = fc1_w.shape[1]
    E = w_gate.shape[1]
    KD, KH, NT = D // P, HID // P, T // P
    HD, RAD = 16, 7
    HS = 4
    QB = P // HS
    NB = T // QB
    KW = 48
    G = 2
    UB = NB // 2
    NP_ = UB // 2
    LEFT = 8
    ZW = LEFT + T + 26
    NCH = 3 * KH
    NX = 2 * KH
    RING = 4

    with ExitStack() as ctx:
        def sb(name, shape, dt=f32):
            return ctx.enter_context(nc.sbuf_tensor(name, shape, dt))

        def pair(name, shape):
            return [sb(f"{name}_hi", shape, f32r), sb(f"{name}_lo", shape, f32r)]
        wqkv = pair("wqkv", [P, KD, 3 * D])
        wproj = pair("wproj", [P, KD, D])
        wf1 = pair("wf1", [P, KD, HID])
        wf2 = pair("wf2", [P, KH, D])
        wm1 = pair("wm1", [P, KD, HID])
        wm2 = pair("wm2", [P, KH, D])
        CW = KD * P + D
        raw = sb("raw", [P, RING, CW])
        wx = pair("wx", [P, RING, CW])
        xin = sb("xin", [P, NT, D])
        y = sb("y", [P, NT, D])
        sx = sb("sx", [P, NT, D])
        acc = sb("acc", [P, NT, D])
        tm = sb("tm", [P, NT, D])
        zT = pair("zT", [P, KD, ZW])
        z3 = pair("z3", [P, KD, T])
        kT = sb("kT", [P, ZW])
        qm = sb("qm", [P, 2, UB, HS * QB])
        kb = sb("kb", [P, 2, UB, G * KW])
        vb = sb("vb", [P, NB // 2, KD * G, P])
        pr = sb("pr", [P, 2, 2, G, 4, 64])
        pT = sb("pT", [P, G, NP_, P])
        zf = [pT[:, g, :, :].rearrange("p j q -> p (j q)") for g in range(G)]
        smax = sb("smax", [P, 2, UB * G])
        rinv = sb("rinv", [P, 4, 2, G, 4])
        hf = sb("hf", [P, 3, T])
        hr = pair("hr", [P, 2, T])
        ident = sb("ident", [P, P])
        band = sb("band", [P, KW])
        hmask = sb("hmask", [P, HS])
        gmask = sb("gmask", [P, G])
        hbias = sb("hbias", [P, KD, HS])
        one = sb("one", [1, 1])
        nil = sb("nil", [1, 1])
        ones = one[:, :].to_broadcast([1, P])
        keep = sb("keep", [P, 3])
        bv = sb("bv", [P, D])
        bproj = sb("bproj", [P, D])
        bfc2 = sb("bfc2", [P, D])
        b2all = sb("b2all", [E + 1, D])
        NSM = E * KH + 2 * KH + 2 * KD + 4 * KD
        small = pT[0:NSM, 0, 0, :]
        smallT = sb("smallT", [P, NSM])
        wg = sb("wg", [P, KD, E])
        bg = sb("bg", [1, E])
        iota = sb("iota", [1, E])
        mhalf = sb("mhalf", [P, 2 * NT])
        st = sb("st", [P, NT, 6])
        mv = sb("mv", [P, 3, NT, 2])
        ve = sb("ve", [P, 2 * NT])
        rs = sb("rs", [P, 4 * NT])
        msum = sb("msum", [P, KD])
        lg = sb("lg", [1, E])
        m8 = sb("m8", [1, 8])
        idx = sb("idx", [1, 8], u32)
        idf = sb("idf", [1, 2])
        tw = sb("tw", [1, 4])
        al = sb("al", [1, 2])
        NR = 3 * E + 3
        rrow = sb("rrow", [1, NR])
        bc = sb("bc", [P, NR])
        cb = sb("cb", [E + 1, 1])
        b1x = sb("b1x", [P, 2, KH])
        b1t = sb("b1t", [P, KH, E])

        psB = ctx.enter_context(nc.psum_tensor("psB", [P, 4, 512], f32))
        psA = ctx.enter_context(nc.psum_tensor("psA", [P, 4, 512], f32))

        oE, oM = 0, E * KH
        oF = oM + KH
        oQK = oF + KH
        oG1 = oQK + 2 * KD
        oB1, oG2, oB2 = oG1 + KD, oG1 + 2 * KD, oG1 + 3 * KD

        p = Plan()
        op = p.op

        def three(eng, dst, a, b, start, stop):
            for n, (u, v) in enumerate(((0, 0), (0, 1), (1, 0))):
                last = eng.matmul(dst, a[u], b[v], start=start and n == 0, stop=stop and n == 2)
            return last

        freed = {b: None for b in range(4)}

        def use(bank, readers):
            freed[bank] = readers

        def bankwait(bank):
            return [(("bank", bank), Back(1))] if freed[bank] is None else list(freed[bank])

        def ffn_weights(n):
            s, e, m = n % RING, n // KH, n % KH

            def load1(sp, row, s=s, e=e, m=m):
                ex = regs[e]
                return sp.dma_start(raw[:, s, 0:KD * P].rearrange("p (k n) -> p k n", k=KD),
                                    W1e[bass.ds(ex, 1), :, m * P:(m + 1) * P].rearrange("a (k p) n -> p (a k) n", p=P))

            def load2(sp, row, s=s, e=e, m=m):
                ex = regs[e]
                return sp.dma_start(raw[:, s, KD * P:], W2e[bass.ds(ex, 1), m * P:(m + 1) * P, :].rearrange("a p n -> p (a n)"))
            free = [("w_hi", n - RING), ("w_lo", n - RING)] if n >= RING else [before("w_hi", NX - RING + n), before("w_lo", NX - RING + n)]
            op("sp", f"raw{s}", (n, 0), load1, free, dma=True)
            op("sp", f"raw{s}", (n, 1), load2, dma=True)

        def ffn_split(n):
            s = n % RING
            free = ("down", KH + n - RING) if n >= RING else before("down", NCH - RING + n)
            op("pool", "w_hi", n, lambda g, r, s=s: g.tensor_scalar(wx[0][:, s, :], raw[:, s, :], 1.0, 0.0, ALU.mult, ALU.add),
               [(f"raw{s}", (n, 1)), free], apart=True)
            op("pool", "w_lo", n, lambda g, r, s=s: g.tensor_tensor(wx[1][:, s, :], raw[:, s, :], wx[0][:, s, :].bitcast(f32), ALU.subtract),
               [("w_hi", n)])

        def chunk_weights(m):
            if m < KH:
                return ([[w[:, k, m * P:(m + 1) * P] for w in wm1] for k in range(KD)], [w[:, m, :] for w in wm2])
            s = (m - KH) % RING
            return ([[w[:, s, k * P:(k + 1) * P] for w in wx] for k in range(KD)], [w[:, s, KD * P:] for w in wx])

        def h_split(kinds, m, pos, fpos, up_key, src, func, bias, h_free, t_free):
            op("act", kinds[0], m, lambda a, r: a.activation(hf[:, fpos, :], src, func, bias=bias), [up_key] + t_free)
            op("act", kinds[1], m, lambda a, r: a.activation(hr[0][:, pos, :], hf[:, fpos, :], ACT.Copy),
               [(kinds[0], m)] + h_free)
            op("dve", kinds[2], m, lambda v, r: v.tensor_tensor(hr[1][:, pos, :], hf[:, fpos, :], hr[0][:, pos, :].bitcast(f32), ALU.subtract),
               [(kinds[1], m)])

        def ffn_up(m):
            w1, _ = chunk_weights(m)
            waits = [("z3_lo", 1)] if m == 0 else []
            if m >= KH:
                waits += [("w_lo", m - KH)]
            waits += [("gelu", m - 2)] if m >= 2 else [before("gelu", NCH - 2 + m)]

            def mm(pe, r, m=m):
                for k in range(KD):
                    last = three(pe, psB[:, m % 2, :], w1[k], [z[:, k, :] for z in z3], k == 0, k == KD - 1)
                return last
            op("pe", "up", m, mm, waits)

        SPLIT = 20
        TR3 = 32
        order = [("f", m) for m in range(SPLIT)] + [("m", m) for m in range(KH)] + [("f", m) for m in range(SPLIT, NCH)]

        def ring_free(q, depth, ffn_kind, mlp_kind):
            me, m = order[q]
            prev, n = order[q - depth]
            if me == "m":
                return [(mlp_kind, n)] if prev == "m" else [before(ffn_kind, n)]
            own = [(ffn_kind, m - depth)] if m >= depth else []
            if q < depth:
                return [before(ffn_kind, NCH - depth + q)]
            return [beside(mlp_kind, n)] + own if prev == "m" else [(ffn_kind, n)]

        def hidden_free(q):
            return ring_free(q, 2, "down", "mdown"), ring_free(q, 3, "h_lo", "mh_lo")

        def ffn_hidden(m, q):
            if m < KH:
                bias = smallT[:, oM + m:oM + m + 1]
            else:
                bias = b1x[:, (m - KH) // KH, m % KH:m % KH + 1]
            h_free, t_free = hidden_free(q)
            h_split(("gelu", "h_hi", "h_lo"), m, q % 2, q % 3, ("up", m), psB[:, m % 2, :], ACT.Gelu_apprx_tanh, bias,
                    h_free, t_free + ([("b1x", 1)] if m == KH else []))

        def ffn_down(m, q):
            _, w2 = chunk_weights(m)
            f, j = divmod(m, KH)

            def tokens(pe, i):
                a = [h[:, q % 2, i * P:(i + 1) * P] for h in hr]
                return three(pe, psB[:, 2 + i // 2, (i % 2) * D:(i % 2 + 1) * D], a, w2,
                             j == 0 and i % 2 == 0, j == KH - 1 and i % 2 == 1)

            taken = [("acc", (f - 1, h)) if f else before("acc", (2, h)) for h in range(2)] if j == 0 else []
            op("pe", "down_1", m, lambda pe, r: [tokens(pe, i) for i in (0, 1)][-1], [("h_lo", m)] + taken[:1])
            op("pe", "down", m, lambda pe, r: [tokens(pe, i) for i in (2, 3)][-1], taken[1:])
            if j == KH - 1:
                for h in range(2):
                    waits = [("down" if h else "down_1", m)] + ([("acc", (f - 1, h))] if f else [("acc0", 0)])
                    c = bc[:, 3 * E + f:3 * E + f + 1]
                    sl = acc[:, 2 * h:2 * h + 2, :].rearrange("p i n -> p (i n)")
                    op("dve", "acc", (f, h), lambda v, r, h=h, c=c, sl=sl: v.scalar_tensor_tensor(
                        sl, psB[:, 2 + h, :], c, sl, ALU.mult, ALU.add), waits)

        regs = {}

        def route_load():
            def load(sp, row):
                for e in range(2):
                    regs[e] = sp.value_load(idx[0:1, e:e + 1], min_val=0, max_val=E - 1)
            op("sp", None, None, lambda sp, row: load(sp, row), [("idx", 0)], apart=True)

        def route_bcast():
            b = 1
            def mm(pe, r):
                pe.matmul(psA[:, b, 0:NR], ones, rrow[:, :], start=True, stop=True)
                return pe.matmul(psA[0:E + 1, b, 256:257], rrow[:, 2 * E:3 * E + 1], one[:, :], start=True, stop=True)
            op("pe", "route1", 0, mm, [("rrow", 6), ("bank", b)])
            op("dve", "cb", 0, lambda v, r: v.tensor_copy(cb[:, :], psA[0:E + 1, b, 256:257]),
               [("route1", 0), before("route2", 0)])
            op("dve", "bc", 0, lambda v, r: v.tensor_copy(bc[:, :], psA[:, b, 0:NR]), [before("acc", (2, 1)), before("b1x", 1)])

        def route_b1():
            for k in range(2):
                op("dve", "b1t", k, lambda v, r, k=k: v.tensor_tensor(
                    b1t[:, :, :], smallT[:, oE:oE + E * KH].rearrange("p (e c) -> p c e", e=E),
                    bc[:, k * E:(k + 1) * E].unsqueeze(1).to_broadcast([P, KH, E]), ALU.mult),
                   [("bc", 0)] + ([("b1x", 0)] if k else []))
                op("dve", "b1x", k, lambda v, r, k=k: v.tensor_reduce(b1x[:, k, :], b1t[:, :, :], AX.X, ALU.add),
                   [("b1t", k), before("gelu", NCH - 1)])

        def route_bias():
            b = 1
            op("pe", "route2", 0, lambda pe, r: pe.matmul(psA[:, b, 0:D], cb[:, :].to_broadcast([E + 1, P]), b2all[:, :], start=True, stop=True),
               [("cb", 0), ("bc", 0)])
            op("dve", "acc0", 0, lambda v, r: v.tensor_tensor(
                acc[:, :, :], sx[:, :, :], psA[:, b, 0:D].unsqueeze(1).to_broadcast([P, NT, D]), ALU.add),
               [("route2", 0), before("store", 1), ("x2", 1)])
            use(b, [before("acc0", 0)])

        def norm_before(kind, n, i):
            return before(kind, (2, i)) if n == 1 else (kind, (1 - n // 2, i))

        def stats(n, src, ready, tiles=range(NT)):
            for i in tiles:
                op("dve", "st", (n, i), lambda v, r, i=i: v.bn_stats(st[:, i, :], src[:, i, :]),
                   (ready if i == tiles[0] else []) + [norm_before("mv", n, i)])
            for i in tiles:
                op("dve", "mv", (n, i), lambda v, r, i=i, n=n: v.bn_aggr(mv[:, n, i, :], st[:, i, :]),
                   [("st", (n, i))] + ([before("rstd", (n, 1))] if i == 0 else []), apart=True)

        def power(n, adds, free, tiles=range(NT)):
            lo, w = tiles[0], len(tiles)
            half = 1 if tiles[-1] == NT - 1 else 0
            at = (0, 2 * NT, 3 * NT)[n] + lo
            for j, (a_, b_) in enumerate(adds):
                op("pool", "vare", (n, half, j), lambda g, r, j=j, a_=a_, b_=b_: g.tensor_scalar(
                    ve[:, j * NT + lo:j * NT + lo + w], mv[:, n, lo:lo + w, 1], a_, b_, ALU.mult, ALU.add),
                   [("mv", (n, tiles[-1])), norm_before("rstd", n, 1)], apart=True)
            wide = w * len(adds)
            op("pool", "rstd", (n, half), lambda g, r: g.tensor_tensor(rs[:, at:at + wide], ve[:, lo:lo + wide], mhalf[:, 0:wide], ALU.pow),
               [("vare", (n, half, len(adds) - 1))] + free)

        HALVES = (range(0, NT // 2), range(NT // 2, NT))

        def norm1_stats():
            stats(0, xin, [("xload", 0)])

        def norm1_power():
            power(0, [(1.0, EPS), (1.0 + EPS, EPS * EPS)], [("y", NT - 1)])

        def norm1_z():
            for i in range(NT):
                op("dve", "z", (0, i), lambda v, r, i=i: v.tensor_scalar(
                    tm[:, i, :], xin[:, i, :], mv[:, 0, i, 0:1], rs[:, NT + i:NT + i + 1], ALU.subtract, ALU.mult),
                   [("rstd", (0, 1)), ("tr3", 1)] if i == 0 else [])

        def first_norm1():
            for i in range(NT):
                op("dve", "st0", i, lambda v, r, i=i: v.bn_stats(st[:, i, :], xin[:, i, :]))
                op("dve", "mv0", i, lambda v, r, i=i: v.bn_aggr(mv[:, 0, i, :], st[:, i, :]), [("st0", i)], apart=True)
            for j, (a_, b_) in enumerate(((1.0, EPS), (1.0 + EPS, EPS * EPS))):
                op("pool", "vare0", j, lambda g, r, j=j, a_=a_, b_=b_: g.tensor_scalar(
                    ve[:, j * NT:(j + 1) * NT], mv[:, 0, :, 1], a_, b_, ALU.mult, ALU.add), [("mv0", NT - 1)], apart=True)
            op("pool", "rstd0", 0, lambda g, r: g.tensor_tensor(rs[:, 0:2 * NT], ve[:, :], mhalf[:, :], ALU.pow), [("vare0", 1)])

        def first_norm1_z():
            for i in range(NT):
                op("dve", "z0", i, lambda v, r, i=i: v.tensor_scalar(
                    tm[:, i, :], xin[:, i, :], mv[:, 0, i, 0:1], rs[:, NT + i:NT + i + 1], ALU.subtract, ALU.mult),
                   [("rstd0", 0)] if i == 0 else [])
            op("pe", None, None, lambda pe, r: None, [("z0", NT - 1)])

        def norm1_y():
            for i in range(NT):
                op("pool", "y", i, lambda g, r, i=i: g.tensor_scalar(
                    y[:, i, :], xin[:, i, :], mv[:, 0, i, 0:1], rs[:, i:i + 1], ALU.subtract, ALU.mult),
                   [before("sx", 0), before("rstd", (0, 1))] if i == 0 else [], apart=True)
            op("pool", "yb", 0, lambda g, r: g.tensor_tensor(
                y[:, :, :], y[:, :, :], bproj[:, :].unsqueeze(1).to_broadcast([P, NT, D]), ALU.add), [("y", NT - 1)])

        def transposes(kind, c, bank, waits):
            def mm(pe, r):
                for i in range(NT):
                    last = pe.transpose(psA[:, bank, i * P:(i + 1) * P], tm[:, i, c * P:(c + 1) * P], ident[:, :])
                return last
            op("pe", kind, c, mm, waits + bankwait(bank))

        def split_T(kind, banks, tr, gain, bias, off, free, zf_free):
            g, b = ([smallT[:, o + c:o + c + 1] for c in range(KD)] for o in (gain, bias))
            op("act", kind + "_f0", 0, lambda a, r: a.activation(zf[0], psA[:, banks[0], :], ACT.Identity, bias=b[0], scale=g[0]),
               [(tr, 0), zf_free(0)])
            op("dve", kind + "_f1", 1, lambda v, r: v.tensor_scalar(zf[1], psA[:, banks[1], :], g[1], b[1], ALU.mult, ALU.add),
               [(tr, 1), zf_free(1)])
            for c in range(KD):
                f = (kind + f"_f{c}", c)
                use(banks[c], [f])
                op("act", kind + "_hi", c, lambda a, r, c=c: a.activation(zT[0][:, c, off:off + T], zf[c], ACT.Copy), [f] + free)
                op("dve", kind + "_lo", c, lambda v, r, c=c: v.tensor_tensor(
                    zT[1][:, c, off:off + T], zf[c], zT[0][:, c, off:off + T].bitcast(f32), ALU.subtract), [(kind + "_hi", c)])

        def split_plain(kind, c, bank, src_key, dst, off, free, accum=None):
            op("act", kind + "_hi", c, lambda a, r: a.activation(dst[0][:, c, off:off + T], psA[:, bank, :], ACT.Identity, accum_out=accum)
               if accum is not None else a.activation(dst[0][:, c, off:off + T], psA[:, bank, :], ACT.Identity),
               [src_key] + free)
            op("dve", kind + "_lo", c, lambda v, r: v.tensor_tensor(
                dst[1][:, c, off:off + T], psA[:, bank, :], dst[0][:, c, off:off + T].bitcast(f32), ALU.subtract),
               [(kind + "_hi", c)])
            use(bank, [(kind + "_lo", c)])

        def tr1():
            for c in range(KD):
                transposes("tr1", c, 2 + c, [before("z", (0, NT - 1))])
            split_T("t1", (2, 3), "tr1", oG1, oB1, LEFT, [before("mup", KH - 1)], lambda c: before("t2_lo", c))

        q_bank, k_bank = (3, 3), (0, 3)

        def project_qk(c, which, bank):
            col = which * D + c * P

            def mm(pe, r):
                for k in range(KD):
                    last = three(pe, psA[:, bank, :], [w[:, k, col:col + P] for w in wqkv],
                                 [z[:, k, LEFT:LEFT + T] for z in zT], k == 0, k == KD - 1)
                return last
            op("pe", "qk", (c, which), mm, [("t1_lo", 1)] + bankwait(bank))

        def keys(c):
            project_qk(c, 1, k_bank[c])
            j = KD + c
            op("act", "kT", c, lambda a, r: a.activation(
                kT[:, LEFT:LEFT + T], psA[:, k_bank[c], :], ACT.Identity, bias=smallT[:, oQK + j:oQK + j + 1]),
               [("qk", (c, 1)), ("kb", (1, 1)) if c else before("kb", (3, 1))])
            use(k_bank[c], [("kT", c)])
            for th in range(2):
                u = 2 * c + th
                first = kT[:, LEFT - RAD + th * UB * QB:LEFT - RAD + th * UB * QB + 1]
                win = bass.AP(first.tensor, first.offset, [first.ap[0], [QB, UB], [1, KW]])
                for g in range(G):
                    op("pool", "kb", (u, g), lambda e, r, th=th, g=g, win=win: e.tensor_scalar(
                        kb[:, th, :, g * KW:(g + 1) * KW], win, gmask[:, g:g + 1], None, ALU.mult),
                       [("kT", c), ("score", (u - 2, 1)) if c else before("score", (u + 2, 1))], apart=True)

        def queries(c):
            project_qk(c, 0, q_bank[c])

        def query_key(u):
            return ("qm_odd" if u % 2 else "qm_even", (u, HS - 1))

        def query_blocks(u):
            c, th = divmod(u, 2)
            free = [("score", (u - 2, 1)) if c else before("score", (u + 2, 1))]
            for s in range(HS):
                dst = qm[:, th, :, s * QB:(s + 1) * QB]
                src = psA[:, q_bank[c], th * UB * QB:(th + 1) * UB * QB].rearrange("p (b q) -> p b q", q=QB)
                if th:
                    op("act", "qm_odd", (u, s), lambda a, r, s=s, src=src, dst=dst: a.activation(
                        dst, src, ACT.Identity, bias=hbias[:, c, s:s + 1], scale=hmask[:, s:s + 1]), [query_key(u - 1)] + free)
                else:
                    op("dve", "qm_even", (u, s), lambda v, r, s=s, src=src, dst=dst: v.tensor_scalar(
                        dst, src, smallT[:, oQK + c:oQK + c + 1], hmask[:, s:s + 1], ALU.add, ALU.mult), [("qk", (c, 0))] + free)
            use(q_bank[c], [query_key(u)])

        def values(n):
            bank = 2

            def mm(pe, r):
                for j in range(2):
                    base = LEFT - RAD + (4 * n + j) * QB
                    for k in range(KD):
                        last = three(pe, psA[:, bank, j * D:(j + 1) * D], [z[:, k, base:base + P] for z in zT],
                                     [w[:, k, 2 * D:] for w in wqkv], k == 0, k == KD - 1)
                return last
            op("pe", "val", n, mm, [("t1_lo", 1)] + bankwait(bank))
            for j in range(2):
                i = 2 * n + j
                kc = 0 if i == 0 else 2 if i == NB // 2 - 1 else 1
                for s in range(2):
                    rows = slice(64 * s, 64 * s + 64)
                    op("dve", "vb", (i, s), lambda v, r, i=i, j=j, s=s, rows=rows, kc=kc: v.scalar_tensor_tensor(
                        vb[rows, i, :, 64 * s:64 * s + 64], bv[rows, :].rearrange("p (g n) -> p g n", n=64),
                        keep[rows, kc:kc + 1], psA[rows, bank, j * D:(j + 1) * D].rearrange("p (g n) -> p g n", n=64),
                        ALU.mult, ALU.add),
                       [("val", n), before("av", (3, 1))])
            use(bank, [("vb", (2 * n + 1, 1))])

        def place(j):
            return 2 * (j % 2) + j // 2

        def score(u, b0):
            th = u % 2
            for h in range(2):
                bank = b0 + h

                def mm(pe, r, h=h, bank=bank):
                    for j in range(4):
                        b = 4 * h + j
                        dst = psA[:, bank, 0:4 * G * KW].rearrange("p (g b k) -> p g b k", g=G, k=KW)[:, :, place(j), :]
                        last = pe.matmul(dst, qm[:, th, b, :], kb[:, th, b, :].rearrange("p (g k) -> p g k", g=G),
                                         start=True, stop=True)
                    return last
                op("pe", "score", (u, h), mm, [query_key(u), ("kb", (u, 1))] + bankwait(bank))
                op("dve", "masked", (u, h), lambda v, r, h=h, bank=bank: v.scalar_tensor_tensor(
                    pr[:, th, h, :, :, 0:KW].rearrange("p g b k -> p (g b) k"),
                    psA[:, bank, 0:4 * G * KW].rearrange("p (n k) -> p n k", k=KW), HD ** -0.5,
                    band[:, :].unsqueeze(1).to_broadcast([P, 4 * G, KW]), ALU.mult, ALU.add),
                   [("score", (u, h)), ("trp", (u - 2, 1)) if u >= 2 else before("trp", (u + 2, 1))])
                use(bank, [("masked", (u, h))])

        def unit_scores(u):
            return pr[:, u % 2, :, :, :, 0:KW].rearrange("p t g b k -> p (t g b) k")

        def shift(u):
            th, s = u % 2, unit_scores(u)
            op("dve", "smax", u, lambda v, r: v.tensor_reduce(smax[:, th, :], s, AX.X, ALU.max), [("masked", (u, 1))])
            op("dve", "shift", u, lambda v, r: v.tensor_tensor(
                s, s, smax[:, th, :].unsqueeze(2).to_broadcast([P, UB * G, KW]), ALU.subtract), [("smax", u)])

        def exp(u):
            s = unit_scores(u)
            op("act", "exp", u, lambda a, r: a.activation(s, s, ACT.Exp), [("shift", u)])

        def sums(u):
            th, s = u % 2, unit_scores(u)
            op("dve", "ssum", u, lambda v, r: v.tensor_reduce(smax[:, th, :], s, AX.X, ALU.add), [("exp", u)])
            op("dve", "rinv", u, lambda v, r: v.reciprocal(
                rinv[:, u, :, :, :].rearrange("p t g b -> p (t g b)"), smax[:, th, :]), [("ssum", u)])

        def probT(u, b0):
            th = u % 2
            for g in range(G):
                bank = b0 + g

                def mm(pe, r, g=g, bank=bank):
                    for j in range(NP_):
                        last = pe.transpose(psA[:, bank, j * P:(j + 1) * P], pr[:, th, j // 2, g, 2 * (j % 2):2 * (j % 2) + 2, :].rearrange("p b k -> p (b k)"), ident[:, :])
                    return last
                op("pe", "trp", (u, g), mm, [("exp", u)] + bankwait(bank))
                op("act", "pT", (u, g), lambda a, r, g=g, bank=bank: a.activation(
                    pT[:, g, :, :].rearrange("p j q -> p (j q)"), psA[:, bank, :], ACT.Copy),
                   [("trp", (u, g)), ("av", (u - 1, g)) if u else before("av", (3, g))])
                use(bank, [("pT", (u, g))])

        def attend(u, b0):
            c, th = divmod(u, 2)
            for g in range(G):
                bank = b0 + g

                def mm(pe, r, g=g, bank=bank):
                    for j in range(NP_):
                        last = pe.matmul(psA[:, bank, j * P:(j + 1) * P], pT[:, g, j, :],
                                         vb[:, th * NP_ + j, c * G + g, :], start=True, stop=True)
                    return last
                op("pe", "av", (u, g), mm, [("pT", (u, g)), ("vb", (th * NP_ + NP_ - 1, 1))] + bankwait(bank))
            for h in range(HS):
                for b in range(P // QB):
                    src = psA[QB * h:QB * h + QB, b0:b0 + 2, :].rearrange(
                        "p g (t j s n) -> p g t j s n", t=2, j=2, s=2)[:, :, :, b % 2, b // 2, HD * h:HD * h + HD]
                    f0 = c * P + HD * h
                    dst = tm[QB * b:QB * b + QB, 2 * th:2 * th + 2, c * P:(c + 1) * P].rearrange(
                        "p t (g n) -> p g t n", g=G)[:, :, :, HD * h:HD * h + HD]
                    w = rinv[QB * h:QB * h + QB, u, :, :, :].rearrange("p t g b -> p g t b")[:, :, :, place(b)]\
                        .unsqueeze(3).to_broadcast([QB, G, 2, HD])
                    op("dve", "att", (u, h, b), lambda v, r, src=src, dst=dst, w=w: v.tensor_tensor(dst, src, w, ALU.mult),
                       [("av", (u, 1)), ("rinv", u), ("tr1", 1)] if (h, b) == (0, 0) else [])
            for g in range(G):
                use(b0 + g, [("att", (u, HS - 1, P // QB - 1))])

        def attT(c, bank):
            transposes("trA", c, bank, [("att", (3, HS - 1, P // QB - 1))])
            split_plain("tA", c, bank, ("trA", c), zT, LEFT, [("val", NB // 4 - 1), ("qk", (1, 0))])

        def project(b0):
            for h in range(2):
                bank = b0 + h

                def mm(pe, r, h=h, bank=bank):
                    for j in range(2):
                        i = 2 * h + j
                        for k in range(KD):
                            last = three(pe, psA[:, bank, j * D:(j + 1) * D],
                                         [z[:, k, LEFT + i * P:LEFT + (i + 1) * P] for z in zT],
                                         [w[:, k, :] for w in wproj], k == 0, k == KD - 1)
                    return last
                op("pe", "proj", h, mm, [("tA_lo", 1)] + bankwait(bank))
                use(bank, [("x1", h)])

        def norm2_stats(b0):
            for h in range(2):
                sl = y[:, 2 * h:2 * h + 2, :].rearrange("p i n -> p (i n)")
                op("dve", "x1", h, lambda v, r, h=h, sl=sl: v.tensor_tensor(sl, sl, psA[:, b0 + h, :], ALU.add),
                   [("proj", h), ("yb", 0)])
                stats(1, y, [("x1", h)], HALVES[h])
                power(1, [(1.0, EPS)], [before("z", (1, NT - 1))], HALVES[h])

        def shortcut():
            op("pool", "sx", 0, lambda g, r: g.tensor_tensor(sx[:, :, :], xin[:, :, :], y[:, :, :], ALU.add),
               [("x1", 1), before("acc0", 0)])
            op("pool", "sxb", 0, lambda g, r: g.tensor_tensor(
                sx[:, :, :], sx[:, :, :], bfc2[:, :].unsqueeze(1).to_broadcast([P, NT, D]), ALU.add), [("sx", 0)])

        def norm2_apply(h):
            for i in HALVES[h]:
                op("dve", "z", (1, i), lambda v, r, i=i: v.tensor_scalar(
                    tm[:, i, :], y[:, i, :], mv[:, 1, i, 0:1], rs[:, 2 * NT + i:2 * NT + i + 1], ALU.subtract, ALU.mult),
                   [("rstd", (1, i * 2 // NT)), ("trA", 1)] if i % 2 == 0 else [])

        def tr2():
            for c in range(KD):
                transposes("tr2", c, c, [("z", (1, NT - 1))])
            split_T("t2", (0, 1), "tr2", oG2, oB2, LEFT, [("proj", 1)], lambda c: ("t1_lo", c))

        def mlp_up(m):
            def mm(pe, r):
                for k in range(KD):
                    last = three(pe, psA[:, m % 2, :], [w[:, k, m * P:(m + 1) * P] for w in wf1],
                                 [z[:, k, LEFT:LEFT + T] for z in zT], k == 0, k == KD - 1)
                return last
            op("pe", "mup", m, mm, [("t2_lo", 1)] + bankwait(m % 2))
            use(m % 2, [("mgelu", m)])

        def mlp_hidden(m, q):
            h_free, t_free = hidden_free(q)
            h_split(("mgelu", "mh_hi", "mh_lo"), m, q % 2, q % 3, ("mup", m), psA[:, m % 2, :], ACT.Gelu,
                    smallT[:, oF + m:oF + m + 1], h_free, t_free)

        def mlp_down(m, q):
            def tokens(pe, i):
                a = [h[:, q % 2, i * P:(i + 1) * P] for h in hr]
                return three(pe, psA[:, 2 + i // 2, (i % 2) * D:(i % 2 + 1) * D], a, [w[:, m, :] for w in wf2],
                             m == 0 and i % 2 == 0, m == KH - 1 and i % 2 == 1)
            op("pe", "mdown_1", m, lambda pe, r: [tokens(pe, i) for i in (0, 1)][-1], [("mh_lo", m)] + (bankwait(2) if m == 0 else []))
            op("pe", "mdown", m, lambda pe, r: [tokens(pe, i) for i in (2, 3)][-1], bankwait(3) if m == 0 else [])
            if m == KH - 1:
                for h in range(2):
                    use(2 + h, [("x2", h)])

        def xload():
            op("sp", "xload", 0, lambda sp, r: sp.dma_start(
                xin[:, :, :], x[bass.ds((r + 1) % ROWS, 1), :, :].rearrange("a (i p) n -> p (a i) n", p=P)),
               [("sx", 0), ("y", NT - 1)], dma=True)

        def norm3_stats():
            for h in range(2):
                sl = sx[:, 2 * h:2 * h + 2, :].rearrange("p i n -> p (i n)")
                op("dve", "x2", h, lambda v, r, h=h, sl=sl: v.tensor_tensor(sl, sl, psA[:, 2 + h, :], ALU.add),
                   [("mdown" if h else "mdown_1", KH - 1), ("sxb", 0)])
                stats(2, sx, [("x2", h)], HALVES[h])
                power(2, [(1.0, EPS)], [before("z", (2, NT - 1))], HALVES[h])

        def norm3_apply():
            for i in range(NT):
                op("dve", "z", (2, i), lambda v, r, i=i: v.tensor_scalar(
                    tm[:, i, :], sx[:, i, :], mv[:, 2, i, 0:1], rs[:, 3 * NT + i:3 * NT + i + 1], ALU.subtract, ALU.mult),
                   [("rstd", (2, i * 2 // NT)), ("tr2", 1)] if i % 2 == 0 else [])

        def tr3(c, bank):
            transposes("tr3", c, bank, [("z", (2, NT - 1))])
            split_plain("z3", c, bank, ("tr3", c), z3, 0, [before("up", NCH - 1), before("router", 0)], msum[:, c:c + 1])

        def router(bank):
            def mm(pe, r):
                for k in range(KD):
                    last = pe.matmul(psA[0:1, bank, 0:E], msum[:, k:k + 1], wg[:, k, :], start=k == 0, stop=k == KD - 1)
                return last
            op("pe", "router", 0, mm, [("z3_hi", 1)] + bankwait(bank))
            use(bank, [("lg", 0)])
            op("dve", "lg", 0, lambda v, r: v.scalar_tensor_tensor(
                lg[:, :], psA[0:1, bank, 0:E], 1.0 / T, bg[:, :], ALU.mult, ALU.add), [("router", 0)])
            op("dve", "m8", 0, lambda v, r: v.max(m8[:, :], lg[:, :]), [("lg", 0)], apart=True)
            op("dve", "idx", 0, lambda v, r: v.max_index(idx[:, :], m8[:, :], lg[:, :]), [("m8", 0), before(f"raw{RING - 1}", (NX - 1, 1))], apart=True)

        def route_row():
            op("dve", "tw", 0, lambda v, r: v.tensor_tensor(tw[:, 0:1], m8[:, 0:1], m8[:, 1:2], ALU.subtract), [("m8", 0)])
            op("act", "tanh", 0, lambda a, r: a.activation(tw[:, 1:2], tw[:, 0:1], ACT.Tanh, scale=0.5), [("tw", 0)])
            op("dve", "idf", 0, lambda v, r: v.tensor_copy(idf[:, :], idx[:, 0:2]), [("idx", 0)])
            for k in range(2):
                op("dve", "rrow", k, lambda v, r, k=k: v.tensor_scalar(
                    rrow[:, k * E:(k + 1) * E], iota[:, :], idf[:, k:k + 1], None, ALU.is_equal),
                   [("idf", 0), before("route1", 0)])
            for k in range(2):
                op("dve", "rrow", 2 + k, lambda v, r, k=k: v.tensor_scalar(
                    tw[:, 2 + k:3 + k], tw[:, 1:2], 0.5 - k, 0.5, ALU.mult, ALU.add), [("tanh", 0)])
            op("dve", "rrow", 4, lambda v, r: v.tensor_scalar(
                rrow[:, 3 * E + 1:3 * E + 3], tw[:, 2:4], al[:, 1:2], None, ALU.mult), [("rrow", 3)])
            op("dve", "rrow", 5, lambda v, r: v.tensor_scalar(
                rrow[:, 2 * E:3 * E], rrow[:, 0:E], rrow[:, 3 * E + 1:3 * E + 2], None, ALU.mult), [("rrow", 4)])
            op("dve", "rrow", 6, lambda v, r: v.scalar_tensor_tensor(
                rrow[:, 2 * E:3 * E], rrow[:, E:2 * E], rrow[:, 3 * E + 2:3 * E + 3], rrow[:, 2 * E:3 * E], ALU.mult, ALU.add),
               [("rrow", 5)])

        pieces = []
        qkv_v = qkv_w.rearrange("(k p) n -> p k n", p=P)
        for k in range(KD):
            for h in range(2):
                c = slice(h * 3 * D // 2, (h + 1) * 3 * D // 2)
                pieces.append((qkv_v[:, k, c], [w[:, k, c] for w in wqkv], None))
        pieces.append((proj_w.rearrange("(k p) n -> p k n", p=P), [w[:, :, :] for w in wproj], KD))

        def first_layer(w, dst):
            v = w.rearrange("(k p) n -> p k n", p=P)
            for k in range(KD):
                for h in range(HID // CW):
                    c = slice(h * CW, (h + 1) * CW)
                    pieces.append((v[:, k, c], [d[:, k, c] for d in dst], None))

        def second_layer(w, dst):
            v = w.rearrange("(m p) n -> p m n", p=P)
            n = CW // D
            for m in range(0, KH, n):
                pieces.append((v[:, m:m + n, :], [d[:, m:m + n, :] for d in dst], n))
        first_layer(fc1_w, wf1)
        second_layer(fc2_w, wf2)
        first_layer(W1m, wm1)
        second_layer(W2m, wm2)

        def raw_piece(n):
            _, dst, inner = pieces[n]
            width = 1
            for d in dst[0].shape[1:]:
                width *= d
            v = raw[:, n % RING, 0:width]
            return v.rearrange("p (k n) -> p k n", k=inner) if inner else v

        start_steps = []
        FIRST = 2 * KD

        def row_loads():
            def row(a):
                return a.rearrange("(o n) -> o n", o=1)
            loads = [(dst[:, :], row(src).to_broadcast([P, D])) for src, dst in ((qkv_b[2 * D:3 * D], bv), (proj_b, bproj), (fc2_b, bfc2))]
            loads += [(b2all[0:E, :], b2e), (b2all[E:E + 1, :], row(b2m)), (wg[:, :, :], w_gate.rearrange("(k p) e -> p k e", p=P)),
                      (bg[:, :], row(b_gate)), (al[:, 0:1], row(alpha))]
            for n, (dst, src) in enumerate(loads):
                op("sp", "rows", n, lambda sp, r, dst=dst, src=src: sp.dma_start(dst, src), dma=True)

        def rows_there():
            for e in ("pe", "dve", "pool"):
                op(e, None, None, lambda eng, r: None, [("rows", 7)])
            for c in range(KD):
                op("dve", "hbias", c, lambda v, r, c=c: v.tensor_scalar(
                    hbias[:, c, :], hmask[:, :], smallT[:, oQK + c:oQK + c + 1], None, ALU.mult))
            op("act", None, None, lambda a, r: None, [("hbias", KD - 1)])
            op("dve", "alpha", 0, lambda v, r: v.tensor_scalar(rrow[:, 3 * E:3 * E + 1], al[:, 0:1], 0.1, 1.0, ALU.max, ALU.min))
            op("dve", "alpha", 1, lambda v, r: v.tensor_scalar(al[:, 1:2], rrow[:, 3 * E:3 * E + 1], -1.0, 1.0, ALU.mult, ALU.add), [("alpha", 0)])
            op("dve", None, None, lambda v, r: None, [("alpha", 1)])

        def zeros():
            op("pool", "zeros", 0, lambda g, r: g.memset(pr[:, :, :, :, :, :], 0.0))
            op("pool", "zeros", 1, lambda g, r: g.memset(vb[:, :, :, :], 0.0))

        def zeros_there():
            op("dve", None, None, lambda v, r: None, [("zeros", 1)])
        start_steps += [rows_there, zeros, zeros_there]

        def split_of(n):
            return ("p_lo" if n < FIRST else "g_lo", n)

        def weights(a, b):
            def f():
                for n in range(a, b):
                    s = n % RING
                    _, dst, _ = pieces[n]
                    op("sp", f"praw{s}", n, lambda sp, r, n=n: sp.dma_start(raw_piece(n), pieces[n][0]),
                       [split_of(n - RING)] if n >= RING else [], dma=True)
                    if n < FIRST:
                        op("act", "p_hi", n, lambda a, r, n=n, dst=dst: a.activation(dst[0], raw_piece(n), ACT.Copy), [(f"praw{s}", n)])
                        op("dve", "p_lo", n, lambda v, r, n=n, dst=dst: v.tensor_tensor(
                            dst[1], raw_piece(n), dst[0].bitcast(f32), ALU.subtract), [("p_hi", n)])
                    else:
                        op("pool", "g_hi", n, lambda g, r, n=n, dst=dst: g.tensor_scalar(
                            dst[0], raw_piece(n), 1.0, 0.0, ALU.mult, ALU.add), [(f"praw{s}", n)], apart=True)
                        op("pool", "g_lo", n, lambda g, r, n=n, dst=dst: g.tensor_tensor(
                            dst[1], raw_piece(n), dst[0].bitcast(f32), ALU.subtract), [("g_hi", n)])
            start_steps.append(f)
            return f

        def ready(n):
            def f():
                op("pe", None, None, lambda pe, r: None, [split_of(n - 1)])
            start_steps.append(f)
            return f

        def table(n, func):
            return lambda: op("act", "table", n, lambda a, r: a.activation(nil[:, :], one[:, :], func),
                              [("table", n - 1) if n else before("table", 2)])

        def both(f, *args):
            return lambda: [f(*a) for a in args]

        GELU_TANH = ACT.Gelu_apprx_tanh
        steps = {
            -1: [table(0, GELU_TANH), route_load, zeros],
            0: [tr1],
            1: [rows_there, route_row, ready(4)],
            2: [both(keys, (0,)), both(queries, (0,)), route_bcast, both(query_blocks, (0,))],
            3: [route_bias, both(query_blocks, (1,)), zeros_there, both(values, (0,))],
            4: [both(score, (0, 0)), both(shift, (0,)), both(values, (1,))],
            5: [both(keys, (1,)), both(score, (1, 0)), both(shift, (1,)), weights(4, 13)],
            6: [both(exp, (0,), (1,)), both(queries, (1,)), both(query_blocks, (2,)), both(sums, (0,)), route_b1],
            7: [both(probT, (0, 0)), both(values, (2,)), both(sums, (1,))],
            8: [norm1_y, both(query_blocks, (3,)), both(score, (2, 0))],
            9: [both(shift, (2,)), both(attend, (0, 2)), both(probT, (1, 0))],
            10: [both(score, (3, 0)), both(values, (3,)), both(shift, (3,))],
            11: [both(exp, (2,), (3,)), both(attend, (1, 2)), weights(13, 17)],
            12: [both(probT, (2, 0)), both(sums, (2,), (3,))],
            13: [both(attend, (2, 2)), both(probT, (3, 0))],
            14: [both(attend, (3, 2))],
            15: [both(attT, (0, 0), (1, 1)), ready(5)],
            16: [both(project, (2,)), both(norm2_stats, (2,)), both(norm2_apply, (0,))],
            17: [both(norm2_apply, (1,))],
            18: [tr2, ready(13)],
            SPLIT - 1: [table(1, ACT.Gelu)],
            SPLIT: [shortcut, weights(17, 21)],
            SPLIT + 3: [xload],
            SPLIT + 6: [norm1_stats, norm1_power],
            SPLIT + 7: [table(2, GELU_TANH)],
            SPLIT + 9: [norm3_stats],
            SPLIT + 10: [norm3_apply],
            TR3: [both(tr3, (0, 0), (1, 1)), norm1_z],
            TR3 + 1: [both(router, (0,))],
        }
        route_steps = (route_load, route_row, route_bcast, route_b1, route_bias)

        def run_steps(s):
            for f in steps.get(s, ()):
                p.stage = "route" if f in route_steps else "start" if f in start_steps else "attn"
                f()

        p.stage = "first"
        first_norm1()
        weights(0, FIRST)()
        p.stage = "second"
        first_norm1_z()
        row_loads()
        run_steps(-1)
        loads = 0
        for q in range(len(order) + 2):
            if q < len(order):
                kind, m = order[q]
                if kind == "f":
                    p.stage = "ffn"
                    while loads < NX and loads < m + RING + 1:
                        ffn_weights(loads)
                        loads += 1
                    if 3 <= m < 3 + RING:
                        ffn_split(m - 3)
                    ffn_up(m)
                else:
                    p.stage = "attn"
                    mlp_up(m)
            if q >= 2:
                kind, m = order[q - 2]
                p.stage = "ffn" if kind == "f" else "attn"
                (ffn_down if kind == "f" else mlp_down)(m, q - 2)
                if kind == "f" and KH <= m < NCH - RING:
                    ffn_split(m - KH + RING)
            if q < len(order):
                kind, m = order[q]
                p.stage = "ffn" if kind == "f" else "attn"
                (ffn_hidden if kind == "f" else mlp_hidden)(m, q)
            run_steps(q)
        p.stage = "start"
        for e in ("pe", "sp"):
            op(e, None, None, lambda eng, r: None, [split_of(len(pieces) - 1)])
        p.stage = "ffn"
        for h in range(2):
            op("sp", "store", h, lambda sp, r, h=h: sp.dma_start(
                out[bass.ds(r, 1), h * T // 2:(h + 1) * T // 2, :].rearrange("a (i p) n -> p (a i) n", p=P),
                acc[:, 2 * h:2 * h + 2, :]), [("acc", (2, h))], dma=True)
        p.final = freed

        sems = {k: ctx.enter_context(nc.semaphore(f"s_{k}")) for k in p.per}
        start = {k: ctx.enter_context(nc.semaphore(f"c_{k}")) for k in
                 ("x", "small", "pool", "dve", "smallT", "smallP")}

        p.idle = ctx.enter_context(nc.semaphore("c_idle"))

        def prime(engine, name):
            for k in p.per:
                if any(o[1] == name and o[2] == k for o in p.ops):
                    engine.sem_inc(sems[k], p.per[k])

        def runs(engine, name):
            p.emit(name, engine, sems, {"start": 0, "attn": 0})
            with engine.Fori(0, ROWS - 1) as i:
                p.emit(name, engine, sems, {"route": i, "ffn": i, "attn": i + 1})
            p.emit(name, engine, sems, {"route": ROWS - 1, "ffn": ROWS - 1}, last=True)

        def first(engine, name, stage="first"):
            p.emit(name, engine, sems, {stage: 0})

        block = ctx.enter_context(nc.Block())

        @block.sync
        def _(sp):
            prime(sp, "sp")

            sp.dma_start(xin[:, :, :], x[0, :, :].rearrange("(i p) n -> p i n", p=P)).then_inc(start["x"], 16)
            first(sp, "sp")
            rows = [(b1e.rearrange("e (c p) -> (e c) p", p=P), oE, E * KH), (b1m.rearrange("(c p) -> c p", p=P), oM, KH),
                    (fc1_b.rearrange("(c p) -> c p", p=P), oF, KH), (qkv_b.rearrange("(c p) -> c p", p=P)[0:2 * KD, :], oQK, 2 * KD),
                    (g1.rearrange("(c p) -> c p", p=P), oG1, KD), (b1.rearrange("(c p) -> c p", p=P), oB1, KD),
                    (g2.rearrange("(c p) -> c p", p=P), oG2, KD), (b2.rearrange("(c p) -> c p", p=P), oB2, KD)]
            for src, at, n in rows:
                sp.dma_start(small[at:at + n, :], src).then_inc(start["small"], 16)
            first(sp, "sp", "second")
            sp.wait_ge(start["smallT"], 1)
            runs(sp, "sp")
            sp.wait_ge(sems["store"], (ROWS + 1) * p.per["store"])

        @block.gpsimd
        def _(g):
            prime(g, "pool")
            n = 0

            def link(ins):
                nonlocal n
                n += 1
                ins.then_inc(start["pool"], 1)
                g.wait_ge(start["pool"], n)
            link(g.memset(mhalf[:, :], -0.5))
            link(g.memset(one[:, :], 1.0))
            link(g.memset(ident[:, :], 0.0))
            link(g.affine_select(out=ident[:, :], in_=ident[:, :], compare_op=ALU.not_equal, fill=1.0, base=0,
                                 pattern=[[-1, P]], channel_multiplier=1))
            first(g, "pool")
            link(g.memset(band[:, :], 0.0))
            for h in range(HS):
                v = band[QB * h:QB * h + QB, :]
                link(g.affine_select(out=v, in_=v, compare_op=ALU.is_ge, fill=-1e30, base=0, pattern=[[1, KW]], channel_multiplier=-1))
                link(g.affine_select(out=v, in_=v, compare_op=ALU.is_ge, fill=-1e30, base=2 * RAD, pattern=[[-1, KW]], channel_multiplier=1))
            link(g.memset(hmask[:, :], 1.0))
            for h in range(2):
                v = hmask[64 * h:64 * h + 64, :]
                link(g.affine_select(out=v, in_=v, compare_op=ALU.is_ge, fill=0.0, base=0, pattern=[[-HD, HS]], channel_multiplier=1))
                link(g.affine_select(out=v, in_=v, compare_op=ALU.is_ge, fill=0.0, base=HD - 1, pattern=[[HD, HS]], channel_multiplier=-1))
            link(g.memset(gmask[:, :], 1.0))
            link(g.affine_select(out=gmask[:, 0:1], in_=gmask[:, 0:1], compare_op=ALU.is_ge, fill=0.0, base=63, pattern=[[0, 1]], channel_multiplier=-1))
            link(g.affine_select(out=gmask[:, 1:2], in_=gmask[:, 1:2], compare_op=ALU.is_ge, fill=0.0, base=-64, pattern=[[0, 1]], channel_multiplier=1))
            link(g.memset(keep[:, :], 1.0))
            link(g.affine_select(out=keep[:, 0:1], in_=keep[:, 0:1], compare_op=ALU.is_ge, fill=0.0, base=-RAD, pattern=[[0, 1]], channel_multiplier=1))
            link(g.affine_select(out=keep[:, 2:3], in_=keep[:, 2:3], compare_op=ALU.is_ge, fill=0.0, base=64 + QB + RAD - 1, pattern=[[0, 1]], channel_multiplier=-1))
            link(g.iota(iota[:, :], pattern=[[1, E]], base=0, channel_multiplier=0, allow_small_or_imprecise_dtypes=True))
            g.wait_ge(start["dve"], len(zT) * 2 + 2)
            runs(g, "pool")
            assert n == N_POOL, n

        @block.vector
        def _(v):
            prime(v, "dve")
            zeros = [kT[:, 0:LEFT], kT[:, LEFT + T:ZW]]
            for z in zT:
                zeros += [z[:, :, 0:LEFT].bitcast(f32), z[:, :, LEFT + T:ZW].bitcast(f32)]
            for z in zeros:
                v.memset(z, 0.0).then_inc(start["dve"], 1)
            v.wait_ge(start["x"], 16)
            first(v, "dve")
            v.wait_ge(start["smallP"], 1)
            v.tensor_copy(smallT[:, :], psA[:, 0, 0:NSM]).then_inc(start["smallT"], 1)
            first(v, "dve", "second")
            v.wait_ge(start["smallT"], 1)
            v.wait_ge(start["pool"], N_POOL)
            runs(v, "dve")

        @block.scalar
        def _(a):
            prime(a, "act")
            first(a, "act")
            a.wait_ge(start["smallT"], 1)
            a.wait_ge(start["pool"], 4)
            a.wait_ge(start["dve"], len(zT) * 2 + 2)
            runs(a, "act")

        @block.tensor
        def _(pe):
            prime(pe, "pe")
            pe.wait_ge(start["small"], 16 * 8)
            pe.wait_ge(start["pool"], 4)
            pe.transpose(psA[:, 0, 0:NSM], small[:, :], ident[0:NSM, 0:NSM]).then_inc(start["smallP"], 1)
            pe.wait_ge(start["smallT"], 1)
            first(pe, "pe", "second")
            runs(pe, "pe")


_INS = ['L0_attn_x', 'L0_attn_qkv_w', 'L0_attn_qkv_b', 'L0_attn_proj_w', 'L0_attn_proj_b', 'L0_attn_norm1_g',
        'L0_attn_norm1_b', 'L0_attn_norm2_g', 'L0_attn_norm2_b', 'L0_attn_fc1_w', 'L0_attn_fc1_b', 'L0_attn_fc2_w',
        'L0_attn_fc2_b', 'L0_ffn_alpha', 'L0_ffn_w_gate', 'L0_ffn_b_gate', 'L0_ffn_W1m', 'L0_ffn_b1m', 'L0_ffn_W2m',
        'L0_ffn_b2m', 'L0_ffn_W1e', 'L0_ffn_b1e', 'L0_ffn_W2e', 'L0_ffn_b2e']


def kernel(**inputs):
    import numpy as np
    import concourse.bacc as bacc
    from concourse.bass_utils import run_bass_kernel_spmd

    nc = bacc.Bacc("TRN2", target_bir_lowering=False, num_devices=1)
    arrays, args = {}, []
    for name in _INS:
        a = np.ascontiguousarray(inputs[name])
        if a.ndim == 0:
            a = a.reshape(1)
        arrays["in_" + name] = a
        args.append(nc.dram_tensor("in_" + name, a.shape, mybir.dt.from_np(a.dtype), kind="ExternalInput").ap())
    shape = arrays["in_L0_attn_x"].shape
    args.append(nc.dram_tensor("out_x", shape, mybir.dt.float32, kind="ExternalOutput").ap())
    build(nc, *args)
    r = run_bass_kernel_spmd(nc, [arrays], core_ids=[0])
    return r.results[0]["out_x"]
```
